# Optimizing a Trainium2 kernel written in Bass

```python
import numpy as np
import jax
import jax.numpy as jnp

def _softmax(x, axis=-1):
    return jax.nn.softmax(x, axis=axis)

def _gelu(x):
    return jax.nn.gelu(x, approximate=True)

def _silu(x):
    return jax.nn.silu(x)

def _sigmoid(x):
    return jax.nn.sigmoid(x)

def _layernorm(x, axis=-1, eps=1e-05):
    m = jnp.mean(x, axis=axis, keepdims=True)
    v = jnp.var(x, axis=axis, keepdims=True)
    return (x - m) / jnp.sqrt(v + eps)

def _scatter_add(tgt, idx, src, axis=0):
    return tgt.at[idx].add(src)

def _segment_sum(src, seg, n):
    return jax.ops.segment_sum(src, seg, n)
kernel_name = 'mk_gnn_resnorm_d2_gnn_r8_713084'

def setup_inputs(seed: int=0):
    np.random.seed(seed)
    _w = jnp.asarray

    def _rec_inputs():
        import jax
        import jax.numpy as jnp
        _gk = jax.random.key(seed)
        x = -0.000202 + 1 * jax.random.normal(jax.random.fold_in(_gk, 1), (6250, 128), jnp.float32)
        _s = jax.random.randint(jax.random.fold_in(_gk, 2), (50000,), 0, 6250, jnp.int32)
        _d = jax.random.randint(jax.random.fold_in(_gk, 3), (50000,), 0, 6250, jnp.int32)
        _loop = jnp.arange(6250, dtype=jnp.int32)
        src = jnp.concatenate([_s, _d, _loop])
        dst = jnp.concatenate([_d, _s, _loop])
        _o = jnp.argsort(dst, stable=True)
        src = src[_o]
        dst = dst[_o]
        edge_attr_128 = -6.47781e-05 + 0.999943 * jax.random.normal(jax.random.fold_in(_gk, 13), (106250, 128), jnp.float32)
        return (x, src, dst, edge_attr_128)
    x, src, dst, edge_attr_128 = _rec_inputs()

    def _L0_gnn_setup():
        import jax, jax.numpy as jnp
        import numpy as np
        N_NODES = 6250
        N_EDGES = 100000
        DIM = 128
        BN_EPS = 1e-05
        key = jax.random.key(seed)
        ks = jax.random.split(key, 12)
        d = DIM
        s = 1.0 / np.sqrt(d)
        x = jax.random.normal(ks[0], (N_NODES, d), dtype=jnp.float32)
        edge_index = jax.random.randint(ks[1], (2, N_EDGES), 0, N_NODES, dtype=jnp.int64)
        W_msg = jax.random.uniform(ks[2], (d, d), jnp.float32, -s, s)
        b_msg = jax.random.uniform(ks[3], (d,), jnp.float32, -s, s)
        sa = 1.0 / np.sqrt(2 * d)
        W_att = jax.random.uniform(ks[4], (2 * d, 1), jnp.float32, -sa, sa)
        b_att = jax.random.uniform(ks[5], (1,), jnp.float32, -sa, sa)
        W_ih = jax.random.uniform(ks[6], (3 * d, d), jnp.float32, -s, s)
        b_ih = jax.random.uniform(ks[7], (3 * d,), jnp.float32, -s, s)
        W_hh = jax.random.uniform(ks[8], (3 * d, d), jnp.float32, -s, s)
        b_hh = jax.random.uniform(ks[9], (3 * d,), jnp.float32, -s, s)
        gamma = jnp.ones((d,), jnp.float32)
        beta = jnp.zeros((d,), jnp.float32)
        return {'x': x, 'edge_index': edge_index, 'W_msg': W_msg, 'b_msg': b_msg, 'W_att': W_att, 'b_att': b_att, 'W_ih': W_ih, 'b_ih': b_ih, 'W_hh': W_hh, 'b_hh': b_hh, 'gamma': gamma, 'beta': beta}
    _L0_gnn_all = _L0_gnn_setup()
    _L0_gnn_in = {k: v for k, v in _L0_gnn_all.items() if k in ('W_msg', 'b_msg', 'W_att', 'b_att', 'W_ih', 'b_ih', 'W_hh', 'b_hh', 'gamma', 'beta')}
    del _L0_gnn_all

    def _L1_gnn_setup():
        import jax, jax.numpy as jnp
        import numpy as np
        N_NODES = 12500
        N_EDGES = 200000
        N_GRAPHS = 50
        F = 128
        key = jax.random.key(seed)
        ks = jax.random.split(key, 10)
        node_features = jax.random.normal(ks[0], (N_NODES, F), dtype=jnp.float32)
        edge_features = jax.random.normal(ks[1], (N_EDGES, F), dtype=jnp.float32)
        global_features = jax.random.normal(ks[2], (N_GRAPHS, F), dtype=jnp.float32)
        W_node = jax.random.normal(ks[3], (F, F), dtype=jnp.float32) / np.sqrt(F)
        W_incoming = jax.random.normal(ks[4], (F, F), dtype=jnp.float32) / np.sqrt(F)
        W_outgoing = jax.random.normal(ks[5], (F, F), dtype=jnp.float32) / np.sqrt(F)
        W_global = jax.random.normal(ks[6], (F, F), dtype=jnp.float32) / np.sqrt(F)
        bias = jax.random.normal(ks[7], (F,), dtype=jnp.float32) / np.sqrt(F)
        receivers = jax.random.randint(ks[8], (N_EDGES,), 0, N_NODES, dtype=jnp.int32)
        senders = jax.random.randint(ks[9], (N_EDGES,), 0, N_NODES, dtype=jnp.int32)
        graph_idx = jnp.repeat(jnp.arange(N_GRAPHS, dtype=jnp.int32), N_NODES // N_GRAPHS)
        return {'node_features': node_features, 'edge_features': edge_features, 'global_features': global_features, 'W_node': W_node, 'W_incoming': W_incoming, 'W_outgoing': W_outgoing, 'W_global': W_global, 'bias': bias, 'receivers': receivers, 'senders': senders, 'graph_idx': graph_idx}
    _L1_gnn_all = _L1_gnn_setup()
    _L1_gnn_in = {k: v for k, v in _L1_gnn_all.items() if k in ('global_features', 'W_node', 'W_incoming', 'W_outgoing', 'W_global', 'bias')}
    del _L1_gnn_all
    return {'x': x, 'src': src, 'dst': dst, 'edge_attr_128': edge_attr_128, 'L0_gnn_W_msg': _L0_gnn_in['W_msg'], 'L0_gnn_b_msg': _L0_gnn_in['b_msg'], 'L0_gnn_W_att': _L0_gnn_in['W_att'], 'L0_gnn_b_att': _L0_gnn_in['b_att'], 'L0_gnn_W_ih': _L0_gnn_in['W_ih'], 'L0_gnn_b_ih': _L0_gnn_in['b_ih'], 'L0_gnn_W_hh': _L0_gnn_in['W_hh'], 'L0_gnn_b_hh': _L0_gnn_in['b_hh'], 'L0_gnn_gamma': _L0_gnn_in['gamma'], 'L0_gnn_beta': _L0_gnn_in['beta'], 'L1_gnn_global_features': _L1_gnn_in['global_features'], 'L1_gnn_W_node': _L1_gnn_in['W_node'], 'L1_gnn_W_incoming': _L1_gnn_in['W_incoming'], 'L1_gnn_W_outgoing': _L1_gnn_in['W_outgoing'], 'L1_gnn_W_global': _L1_gnn_in['W_global'], 'L1_gnn_bias': _L1_gnn_in['bias']}

def reference(x, src, dst, edge_attr_128, L0_gnn_W_msg, L0_gnn_b_msg, L0_gnn_W_att, L0_gnn_b_att, L0_gnn_W_ih, L0_gnn_b_ih, L0_gnn_W_hh, L0_gnn_b_hh, L0_gnn_gamma, L0_gnn_beta, L1_gnn_global_features, L1_gnn_W_node, L1_gnn_W_incoming, L1_gnn_W_outgoing, L1_gnn_W_global, L1_gnn_bias):
    import jax
    import jax.numpy as jnp

    def _L0_gnn_ref(x, edge_index, W_msg, b_msg, W_att, b_att, W_ih, b_ih, W_hh, b_hh, gamma, beta):
        import jax, jax.numpy as jnp
        import numpy as np
        N_NODES = 6250
        N_EDGES = 100000
        DIM = 128
        BN_EPS = 1e-05
        num_nodes, d = x.shape
        src = edge_index[0]
        dst = edge_index[1]
        xs = x[src]
        xd = x[dst]
        att = jax.nn.sigmoid(xs @ W_att[:d] + xd @ W_att[d:] + b_att)
        messages = (xs @ W_msg + b_msg) * att
        aggregated = jax.ops.segment_sum(messages, dst, num_segments=num_nodes)
        gi = aggregated @ W_ih.T + b_ih
        gh = x @ W_hh.T + b_hh
        i_r, i_z, i_n = jnp.split(gi, 3, axis=1)
        h_r, h_z, h_n = jnp.split(gh, 3, axis=1)
        r = jax.nn.sigmoid(i_r + h_r)
        z = jax.nn.sigmoid(i_z + h_z)
        n = jnp.tanh(i_n + r * h_n)
        h_new = (1.0 - z) * n + z * x
        mean = jnp.mean(h_new, axis=0)
        var = jnp.var(h_new, axis=0)
        return gamma * (h_new - mean) * jax.lax.rsqrt(var + BN_EPS) + beta

    def _L1_gnn_ref(node_features, edge_features, global_features, W_node, W_incoming, W_outgoing, W_global, bias, receivers, senders, graph_idx):
        import jax, jax.numpy as jnp
        import numpy as np
        N_NODES = 12500
        N_EDGES = 200000
        N_GRAPHS = 50
        F = 128
        n_nodes = node_features.shape[0]
        new_nodes = node_features @ W_node.T
        agg_in = jax.ops.segment_sum(edge_features, receivers, num_segments=n_nodes)
        new_nodes = new_nodes + agg_in @ W_incoming.T
        agg_out = jax.ops.segment_sum(edge_features, senders, num_segments=n_nodes)
        new_nodes = new_nodes + agg_out @ W_outgoing.T
        glob_proj = global_features @ W_global.T
        new_nodes = new_nodes + glob_proj[graph_idx]
        new_nodes = new_nodes + bias
        return new_nodes
    edge_index = jnp.stack([src, dst])
    batch0 = jnp.zeros((6250,), jnp.int32)
    x = _layernorm(x + _L0_gnn_ref(x, edge_index, L0_gnn_W_msg, L0_gnn_b_msg, L0_gnn_W_att, L0_gnn_b_att, L0_gnn_W_ih, L0_gnn_b_ih, L0_gnn_W_hh, L0_gnn_b_hh, L0_gnn_gamma, L0_gnn_beta), axis=-1)
    x = _layernorm(x + _L1_gnn_ref(x, edge_attr_128, L1_gnn_global_features, L1_gnn_W_node, L1_gnn_W_incoming, L1_gnn_W_outgoing, L1_gnn_W_global, L1_gnn_bias, dst, src, batch0), axis=-1)
    return x

_drawn_inputs = setup_inputs


def setup_inputs(seed=0):
    import zlib

    import numpy as np

    out = dict(_drawn_inputs(seed))
    spreads = {'L0_gnn_gamma': (1.0, 0.6), 'L0_gnn_beta': (0.0, 0.611)}
    factors = {'L0_gnn_b_msg': 3.822,
     'L0_gnn_W_att': 3.626,
     'L0_gnn_b_ih': 8.0,
     'L0_gnn_b_hh': 21.865,
     'L1_gnn_bias': 3.559}
    for name, (base, spread) in spreads.items():
        noise = np.random.default_rng([zlib.crc32(name.encode()), seed]).standard_normal(out[name].shape)
        drawn = base * np.exp(spread * noise) if base else spread * noise
        out[name] = jnp.asarray(drawn.astype(out[name].dtype))
    for name, factor in factors.items():
        out[name] = (out[name] * factor).astype(out[name].dtype)
    return out
```

```python
from contextlib import ExitStack

import concourse.bass as bass
from concourse import mybir

ALU = mybir.AluOpType
ACT = mybir.ActivationFunctionType
AX = mybir.AxisListType
F32 = mybir.dt.float32
I32 = mybir.dt.int32
U32 = mybir.dt.uint32

P = 128
TPC = 8
CHUNK = P * TPC
SLOTS = 4
GROUP = 4
TABLES = 4
BANK = 512
GW = 250
AW = 500
EPS = 1e-5
FAR = 20000.0


def gnn_two_layers(nc, x, xT, src, dst, edge_attr, W_msg, b_msg, W_att, b_att, W_ihT, b_ih, W_hhT, b_hh,
                   gamma, beta, glob, W_nodeT, W_inT, W_outT, W_globT, bias, out):
    N = x.shape[0]
    E = edge_attr.shape[0]
    NC = -(-E // CHUNK)
    WHOLE = NC - 1
    LAST = E - CHUNK
    DONE = WHOLE * CHUNK - LAST
    NB = -(-N // P)
    NPAD = (NB + 1) * P
    TRASH = NB * P
    MASKED = TRASH + P
    ROWS = MASKED + 2 * P
    GS = N // GW
    PAIRS = NC // 2
    AS = N // AW
    ITERS = NC // SLOTS
    assert NC % SLOTS == 0 and N % GW == 0 and GS % 2 == 1 and NC <= P and DONE <= 2 * P
    NG = NB // GROUP
    assert N - AS * AW == GW and AS % 2 == 0 and ROWS % P == 0 and NB % GROUP == 1 and NG % SLOTS == 0
    assert NC % 4 == 0 and 2 * GS + 2 == PAIRS and TABLES == 4

    with ExitStack() as ctx:
        def sb(name, shape, dt=F32):
            return ctx.enter_context(nc.sbuf_tensor(name, shape, dt))

        def sem(name):
            return ctx.enter_context(nc.semaphore(name))

        ps = ctx.enter_context(nc.psum_tensor("ps", [P, 8, BANK], F32))

        tables = [nc.dram_tensor(f"by_src_{k}", [ROWS, P], F32, kind="Internal").ap() for k in range(TABLES)]

        iota_i = sb("iota_i", [P, P], I32)
        part_i = sb("part_i", [P, 1], I32)
        col = sb("col", [P, P])
        part = sb("part", [P, 1])
        trash_row = sb("trash_row", [P, 1])
        ident = sb("ident", [P, P])
        earlier = sb("earlier", [P, P])
        ones = sb("ones", [P, P])
        mean_w = sb("mean_w", [P, P])
        center = sb("center", [P, P])
        eps = sb("eps", [P, 1])

        base_i = sb("base_i", [1, NC], I32)
        gather_all = sb("gather_all", [P, NC + SLOTS, TPC], U32)
        rel = sb("rel", [P, NC, TPC])
        key = sb("key", [P, NC + 2, TPC])
        key_now = sb("key_now", [P, 2, TPC])
        n_left = sb("n_left", [P, 1])
        n_left_i = sb("n_left_i", [1, 1], I32)
        gather_idx = sb("gather_idx", [P, SLOTS, TPC], U32)
        scatter_idx = sb("scatter_idx", [P, SLOTS, TPC], U32)

        xT_sb = sb("xT_sb", [P, NB * P])
        by_node = xT_sb[:].rearrange("p (b f) -> p b f", f=P)
        w_att_sb = sb("w_att_sb", [P, 2])
        diag = sb("diag", [P, 2, P])
        w_att_a = sb("w_att_a", [P, P])
        b_att_sb = sb("b_att_sb", [P, 1])
        w_msg_sb = sb("w_msg_sb", [P, P])
        b_msg_row = sb("b_msg_row", [1, P])
        w_ih_sb = sb("w_ih_sb", [P, 3 * P])
        w_hh_sb = sb("w_hh_sb", [P, 3 * P])
        b_ih_sb = sb("b_ih_sb", [P, 3])
        b_hh_sb = sb("b_hh_sb", [P, 3])
        b_gate = sb("b_gate", [P, 2])
        vecs = sb("vecs", [P, 4])
        w_glob_sb = sb("w_glob_sb", [P, P])
        w_node_sb = sb("w_node_sb", [P, P])
        w_in_sb = sb("w_in_sb", [P, P])
        w_out_sb = sb("w_out_sb", [P, P])
        bias_all = sb("bias_all", [P, P])

        dst_term = sb("dst_term", [P, NPAD])
        acc_x = sb("acc_x", [P, NPAD])
        acc_w = sb("acc_w", [1, NPAD])
        acc_in = sb("acc_in", [P, NPAD])

        rows = sb("rows", [P, SLOTS, TPC, P])
        ea = sb("ea", [P, 2, TPC, P])
        src_term = sb("src_term", [P, 2, TPC])
        att = sb("att", [P, SLOTS, TPC, P])
        hot = sb("hot", [P, 2, TPC, P])
        same = sb("same", [P, TPC, P])
        dups = sb("dups", [P, TPC, P])
        n_dups = sb("n_dups", [P, TPC])
        moved = sb("moved", [P, TPC])
        to_trash = sb("to_trash", [P, TPC])
        stats = sb("stats", [P, GS * 6])
        bn = sb("bn", [P, 7])
        bn_mean, bn_var, bn_std, bn_inv, bn_scale, bn_off, bn_shift = (bn[:, k:k + 1] for k in range(7))

        src_rows, rel_rows, key_rows, mask_rows = (acc_x[0:NC, k * CHUNK:(k + 1) * CHUNK] for k in range(4))
        hot_c = hot[0:NC].rearrange("c s j f -> c s (j f)")
        src_rows_i, dst_rows_i = (hot_c[:, s].bitcast(I32) for s in range(2))
        att_c = att[0:NC].rearrange("c s j f -> c s (j f)")
        mask_i, number_i = (att_c[:, s].bitcast(I32) for s in range(2))
        base_col = n_dups[0:NC, 0:1]

        agg, reset, update, new, pre, tmp, sq, y = (dst_term[:, k * GW:(k + 1) * GW] for k in range(8))
        D = 8 * GW
        z_sb, sums_T, biased, normed = (
            dst_term[:, D + k * 2 * BANK:D + (k + 1) * 2 * BANK].rearrange("p (h b f) -> p h b f", h=2, f=P) for k in range(4))
        o_stat = hot[:, 0, 0, 0:2 * GROUP * 6].rearrange("p (h b k) -> p h b k", h=2, k=6)
        o_mv = hot[:, 0, 1, 0:2 * GROUP * 2].rearrange("p (h b k) -> p h b k", h=2, k=2)
        o_std, o_inv, o_shift = (hot[:, 0, 2 + k, 0:2 * GROUP].rearrange("p (h b) -> p h b", h=2) for k in range(3))
        tabs = [buf[:, 2 * h:2 * h + 2].rearrange("p s j f -> p (s j) f").rearrange("p (k b) f -> p k b f", k=TABLES)
                for buf in (rows, att) for h in range(2)]
        base_bc = dups[:, 0, 0:NC]
        base_f = dups[0:1, 1, 0:NC]
        left_now = moved[:]
        left = ea[:, 1].rearrange("p j f -> p (j f)")[:, 0:NC * TPC].rearrange("p (c j) -> p c j", j=TPC)

        att_loaded = sem("att_loaded")
        iotas_made, consts_made = sem("iotas_made"), sem("consts_made")
        idx_loaded, w_loaded, x_loaded = sem("idx_loaded"), sem("w_loaded"), sem("x_loaded")
        idx_kept, acc_x_zero = sem("idx_kept"), sem("acc_x_zero")
        rows_made, rows_turned, idx_made = sem("rows_made"), sem("rows_turned"), sem("idx_made")
        att_diag_made, att_spread, att_kept, weights_made, bias_spread, bias_kept = (
            sem(n) for n in ("att_diag_made", "att_spread", "att_kept", "weights_made", "bias_spread", "bias_kept"))
        dst_term_ps, dst_term_sb, accs_zero = sem("dst_term_ps"), sem("dst_term_sb"), sem("accs_zero")
        left_step, left_counted, left_known = sem("left_step"), sem("left_counted"), sem("left_known")
        gather_idx_made = sem("gather_idx_made")
        gathered = [sem(f"gathered{s}") for s in range(SLOTS)]
        src_term_made, att_made, hot_made = sem("src_term_made"), sem("att_made"), sem("hot_made")
        summed, added = sem("summed"), sem("added")
        g_base, g_base_ps, g_left, g_ready, g_loaded, g_gathered = (
            sem(n) for n in ("g_base", "g_base_ps", "g_left", "g_ready", "g_loaded", "g_gathered"))
        g_src_term, g_hot, g_att, g_weighted, g_summed, g_added = (
            sem(n) for n in ("g_src_term", "g_hot", "g_att", "g_weighted", "g_summed", "g_added"))
        by_dst_done = sem("by_dst_done")
        zeros_made = sem("zeros_made")
        table_free = [sem(f"table_free{k}") for k in range(TABLES)]
        ea_loaded = [sem(f"ea_loaded{q}") for q in range(2)]
        keys_copied, keys_spread, onehot_made, same_made, dups_made = (
            sem(n) for n in ("keys_copied", "keys_spread", "onehot_made", "same_made", "dups_made"))
        counted, moved_made, scatter_idx_made = sem("counted"), sem("moved_made"), sem("scatter_idx_made")
        in_summed, in_added, merged, merged_kept = (
            sem("in_summed"), sem("in_added"), sem("merged"), sem("merged_kept"))
        scattered = sem("scattered")
        agg_ps, agg_sb, gates_ps, reset_made, update_made, scaled, pre_made, new_made, diff_made, mixed, h_made, bn_stats_made = (
            sem(n) for n in ("agg_ps", "agg_sb", "gates_ps", "reset_made", "update_made", "scaled", "pre_made", "new_made",
                             "diff_made", "mixed", "h_made", "bn_stats_made"))
        bn_made = [sem(f"bn_made{k}") for k in range(7)]
        u_made, y_made, centered, squared, var_ps, std_made, inv_made, x1_made = (
            sem(n) for n in ("u_made", "y_made", "centered", "squared", "var_ps", "std_made", "inv_made", "x1_made"))
        tabs_loaded = [sem(f"tabs_loaded{s}") for s in range(SLOTS)]
        z_ps, z_kept, z_turned, z_added = (sem(n) for n in ("z_ps", "z_kept", "z_turned", "z_added"))
        tabs_halved, tabs_summed, tabs_kept, out_ps = (
            sem(n) for n in ("tabs_halved", "tabs_summed", "tabs_kept", "out_ps"))
        o_added, o_stats_made, o_mv_made, o_std_made, o_inv_made, o_shift_made, o_made = (
            sem(n) for n in ("o_added", "o_stats_made", "o_mv_made", "o_std_made", "o_inv_made", "o_shift_made", "o_made"))
        stored = [sem(f"stored{h}") for h in range(2)]

        turned = ps[:, 0:6, 0:4 * NC].rearrange("p b (j c) -> p b j c", c=NC)
        base_ps = ps[0:1, 6, 0:NC]
        spread_ps = ps[:, 7, 0:2 * P].rearrange("p (v f) -> p v f", v=2)
        sum_ps = [ps[:, q, 0:P] for q in range(2)]
        weight_ps = [ps[0:1, 2 + q, 0:P] for q in range(2)]
        key_ps = ps[:, 0:2].rearrange("p b (j f) -> p (b j) f", f=P)
        in_ps = ps[:, 2, 0:P]
        merge_ps = ps[:, 3:5].rearrange("p b (j f) -> p (b j) f", f=P)
        agg_bank, reset_bank, update_bank = ps[:, 5, 0:GW], ps[:, 5, GW:2 * GW], ps[:, 6, 0:GW]
        new_in_bank, new_h_bank = ps[:, 7, 0:GW], ps[:, 7, GW:2 * GW]
        center_bank, var_bank = ps[:, 5, 0:GW], ps[:, 6, 0:GW]

        turned_z = [ps[:, 2 + h].rearrange("p (b f) -> p b f", f=P) for h in range(2)]
        summed_T = [ps[:, 4 + h].rearrange("p (b f) -> p b f", f=P) for h in range(2)]
        out_bank = [ps[:, 6 + h].rearrange("p (b f) -> p b f", f=P) for h in range(2)]

        def chunk_of(array, c):
            return array[:, bass.ds(c, 1)].rearrange("p c j -> p (c j)")

        block = ctx.enter_context(nc.Block())
        N_W = 18

        @block.sync
        def _(sp):
            sp.dma_start(src_rows_i[0:WHOLE], src[0:WHOLE * CHUNK].rearrange("(c e) -> c e", e=CHUNK)).then_inc(idx_loaded, 16)
            sp.dma_start(dst_rows_i[0:WHOLE], dst[0:WHOLE * CHUNK].rearrange("(c e) -> c e", e=CHUNK)).then_inc(idx_loaded, 16)
            sp.dma_start(src_rows_i[WHOLE:NC], src[LAST:E].rearrange("(c e) -> c e", c=1)).then_inc(idx_loaded, 16)
            sp.dma_start(dst_rows_i[WHOLE:NC], dst[LAST:E].rearrange("(c e) -> c e", c=1)).then_inc(idx_loaded, 16)
            sp.dma_start(xT_sb[:, 0:N], xT).then_inc(x_loaded, 16)

            def edges_from(first_edge):
                return edge_attr[bass.ds(first_edge, CHUNK)].rearrange("(p j) f -> p j f", j=TPC)

            sp.wait_ge(accs_zero, 1)
            sp.wait_ge(hot_made, 1)
            for k in range(TABLES):
                flat = tables[k].rearrange("(p a) f -> p (a f)", p=P)
                sp.dma_start(flat[:, 0:NPAD], acc_in[:]).then_inc(zeros_made, 16)
                sp.dma_start(flat[:, NPAD:ROWS], acc_in[:, 0:ROWS - NPAD]).then_inc(zeros_made, 16)

            sp.wait_ge(left_known, 1)
            with sp.If(sp.value_load(n_left_i[0:1, 0:1], min_val=0, max_val=E) > 0):
                with sp.Fori(0, WHOLE) as c:
                    sp.wait_ge(g_ready, c + 1)
                    sp.dma_start(ea[:, 0], edges_from(c * CHUNK)).then_inc(g_loaded, 16)
                sp.wait_ge(g_ready, NC)
                sp.dma_start(ea[:, 0], edges_from(LAST)).then_inc(g_loaded, 16)
                sp.wait_ge(g_added, NC * NB)

            def load(q, c, first_edge):
                sp.dma_start(ea[:, q], edges_from(first_edge)).then_inc(ea_loaded[q], 16)

            load(0, 0, 0)
            load(1, 1, CHUNK)
            with sp.Fori(1, PAIRS - 1) as i:
                for q in range(2):
                    sp.wait_ge(merged, 2 * i + (q - 1))
                    load(q, 2 * i + q, i * (2 * CHUNK) + q * CHUNK)
            sp.wait_ge(merged, NC - 3)
            load(0, NC - 2, (NC - 2) * CHUNK)
            sp.wait_ge(merged, NC - 2)
            load(1, NC - 1, LAST)

            def load_tables(s, g, blocks):
                for k in range(TABLES):
                    sp.dma_start(tabs[s][:, k, 0:blocks],
                                 tables[k][bass.ds(g * (GROUP * P), blocks * P)].rearrange("(b p) f -> p b f", p=P)
                                 ).then_inc(tabs_loaded[s], 16)

            for k in range(TABLES):
                sp.wait_ge(table_free[k], 16 * (NC * TPC // TABLES))
            for s in range(SLOTS):
                load_tables(s, s, GROUP)
            with sp.Fori(1, NG // SLOTS) as i:
                for s in range(SLOTS):
                    sp.wait_ge(tabs_summed, SLOTS * i + (s + 1 - SLOTS))
                    load_tables(s, i * SLOTS + s, GROUP)
            sp.wait_ge(tabs_summed, NG + 1 - SLOTS)
            load_tables(0, NG, 1)

        @block.gpsimd
        def _(pool):
            nc.gpsimd.iota(iota_i[:], [[1, P]], base=0, channel_multiplier=0)
            nc.gpsimd.iota(part_i[:], [[1, 1]], base=0, channel_multiplier=1)
            nc.gpsimd.iota(mask_i, [[1, CHUNK]], base=WHOLE * CHUNK - DONE, channel_multiplier=-CHUNK)
            nc.gpsimd.iota(number_i, [[1, CHUNK]], base=MASKED, channel_multiplier=0).then_inc(iotas_made, 1)
            nc.gpsimd.memset(acc_in[:], 0.0)
            nc.gpsimd.memset(acc_w[:], 0.0).then_inc(accs_zero, 1)

            def gather(s, done):
                for j in range(TPC):
                    pool.indirect_dma_start(rows[:, s, j, :], None, x,
                                            bass.IndirectOffsetOnAxis(ap=gather_idx[:, s, j:j + 1], axis=0)
                                            ).then_inc(done, 16)

            pool.wait_ge(gather_idx_made, SLOTS)
            for s in range(SLOTS):
                gather(s, gathered[s])
            with pool.Fori(1, ITERS) as i:
                for s in range(SLOTS):
                    pool.wait_ge(summed, SLOTS * i + (s + 1 - SLOTS))
                    pool.nop(nofuse=True)
                    pool.wait_ge(gather_idx_made, SLOTS * i + s + 1)
                    pool.nop(nofuse=True)
                    gather(s, gathered[s])

            pool.wait_ge(left_known, 1)
            with pool.If(pool.value_load(n_left_i[0:1, 0:1], min_val=0, max_val=E) > 0):
                with pool.Fori(0, NC) as c:
                    pool.wait_ge(g_ready, c + 1)
                    pool.nop(nofuse=True)
                    gather(0, g_gathered)

            pool.wait_ge(zeros_made, 2 * 16 * TABLES)

            def scatter(s, c, first):
                pool.wait_ge(scatter_idx_made, c + 1)
                pool.nop(nofuse=True)
                pool.wait_ge(merged_kept, c + 1)
                pool.nop(nofuse=True)
                for j in range(TPC):
                    k, turn = j % TABLES, j // TABLES
                    if not (first and turn == 0):
                        pool.wait_ge(table_free[k], c * (16 * TPC // TABLES) + 16 * turn)
                        pool.nop(nofuse=True)
                    pool.indirect_dma_start(tables[k], bass.IndirectOffsetOnAxis(ap=scatter_idx[:, s, j:j + 1], axis=0),
                                            att[:, s, j, :], None, compute_op=ALU.add).then_inc(table_free[k], 16)
                    if j == TABLES - 1:
                        pool.sem_inc(scattered, 1)

            for s in range(SLOTS):
                scatter(s, s, s == 0)
            with pool.Fori(1, ITERS) as i:
                for s in range(SLOTS):
                    scatter(s, SLOTS * i + s, False)

            def halve(s, i, g, blocks):
                pool.wait_ge(tabs_loaded[s], i * (16 * TABLES) + 16 * TABLES)
                nc.gpsimd.tensor_tensor(tabs[s][:, 0:2, 0:blocks], tabs[s][:, 0:2, 0:blocks], tabs[s][:, 2:4, 0:blocks], ALU.add
                                        ).then_inc(tabs_halved, 1)

            with pool.Fori(0, NG // SLOTS) as i:
                for s in range(SLOTS):
                    halve(s, i, SLOTS * i + s, GROUP)
            halve(0, NG // SLOTS, NG, 1)

        @block.scalar
        def _(act):
            def column(a):
                return a.rearrange("(p o) -> p o", o=1)

            for o, a in ((w_att_sb[:, 0:1], W_att[0:P]), (w_att_sb[:, 1:2], W_att[P:2 * P]),
                         (b_att_sb[:], b_att.rearrange("(o d) -> o d", o=1).to_broadcast([P, 1]))):
                act.dma_start(o, a).then_inc(att_loaded, 16)
            for o, a in ((w_msg_sb[:], W_msg), (b_msg_row[:], b_msg.rearrange("(o d) -> o d", o=1)),
                         (w_ih_sb[:], W_ihT), (w_hh_sb[:], W_hhT),
                         (vecs[:, 0:1], column(gamma)), (vecs[:, 1:2], column(beta)),
                         (vecs[:, 2:3], column(glob[0])), (vecs[:, 3:4], column(bias)),
                         (w_glob_sb[:], W_globT), (w_node_sb[:], W_nodeT), (w_in_sb[:], W_inT), (w_out_sb[:], W_outT),
                         *[(b_ih_sb[:, g:g + 1], column(b_ih[g * P:(g + 1) * P])) for g in range(3)],
                         *[(b_hh_sb[:, g:g + 1], column(b_hh[g * P:(g + 1) * P])) for g in range(3)]):
                act.dma_start(o, a).then_inc(w_loaded, 16)

            act.wait_ge(att_loaded, 16 * 3)

            def keep_dst_term(q, t, width):
                act.wait_ge(dst_term_ps, t + 1)
                nc.scalar.activation(dst_term[:, bass.ds(t * AW, width)], ps[:, q, 0:width], ACT.Identity,
                                     bias=b_att_sb[:, 0:1]).then_inc(dst_term_sb, 1)

            with act.Fori(0, AS // 2) as i:
                for q in range(2):
                    keep_dst_term(q, 2 * i + q, AW)
            keep_dst_term(0, AS, GW)

            def weights(q, src_terms, first_node, done):
                for j in range(TPC):
                    last = nc.scalar.activation(att[:, q, j, :], dst_term[:, bass.ds(first_node, P)], ACT.Sigmoid,
                                                bias=src_terms[:, j:j + 1])
                last.then_inc(done, 1)

            act.wait_ge(idx_made, 1)
            act.wait_ge(dst_term_sb, AS + 1)
            with act.Fori(0, PAIRS) as i:
                for q in range(2):
                    c = 2 * i + q
                    first = act.value_load(base_i[0:1, bass.ds(c, 1)], min_val=0, max_val=N - 1)
                    act.wait_ge(src_term_made, c + 1)
                    weights(q, src_term[:, q], first, att_made)

            act.wait_ge(left_known, 1)
            with act.If(act.value_load(n_left_i[0:1, 0:1], min_val=0, max_val=E) > 0):
                with act.Fori(0, NC) as c:
                    with act.Fori(0, NB) as b:
                        act.wait_ge(g_hot, c * NB + b + 1)
                        weights(0, src_term[:, 0], b * P, g_att)
            act.wait_ge(by_dst_done, 1)

            def keep(s, c, first_quad):
                if not first_quad:
                    act.wait_ge(scattered, c - 2)
                act.wait_ge(merged, c + 1)
                for h in range(2):
                    last = nc.scalar.activation(att[:, s, 4 * h:4 * h + 4, :], merge_ps[:, 4 * h:4 * h + 4, :], ACT.Copy)
                last.then_inc(merged_kept, 1)

            def gru_head(t):
                act.wait_ge(agg_ps, t + 1)
                nc.scalar.activation(agg, agg_bank, ACT.Copy).then_inc(agg_sb, 1)

            def gru_gates(t, first):
                act.wait_ge(gates_ps, t + 1)
                if not first:
                    act.wait_ge(h_made, t)
                nc.scalar.activation(reset, reset_bank, ACT.Sigmoid, bias=b_gate[:, 0:1]).then_inc(reset_made, 1)
                nc.scalar.activation(update, update_bank, ACT.Sigmoid, bias=b_gate[:, 1:2]).then_inc(update_made, 1)

            def gru_new(t):
                act.wait_ge(pre_made, t + 1)
                nc.scalar.activation(new, pre, ACT.Tanh, bias=b_ih_sb[:, 2:3]).then_inc(new_made, 1)

            def pair_with_gru(p, h, back, first_quad):
                if back >= 1:
                    gru_gates(p - 1, back == 1)
                keep(2 * h, 2 * p, first_quad)
                if back >= 1:
                    gru_new(p - 1)
                gru_head(p)
                keep(2 * h + 1, 2 * p + 1, first_quad)

            act.wait_ge(weights_made, 1)
            pair_with_gru(0, 0, 0, True)
            pair_with_gru(1, 1, 1, True)
            with act.Fori(1, GS // 2) as i:
                for h in range(2):
                    pair_with_gru(2 * i + h, h, 2, False)
            pair_with_gru(GS - 1, 0, 2, False)
            gru_gates(GS - 1, False)
            gru_new(GS - 1)

            act.wait_ge(bn_made[0], 1)
            nc.scalar.activation(bn_std, bn_var, ACT.Sqrt, bias=eps[:, 0:1]).then_inc(bn_made[1], 1)
            act.wait_ge(bn_made[5], 1)

            u, std = agg, reset

            def pair_with_ln(t, h, first):
                if not first:
                    act.wait_ge(y_made, t)
                nc.scalar.activation(u, acc_x[:, bass.ds(t * GW, GW)], ACT.Identity, scale=bn_scale, bias=bn_shift
                                     ).then_inc(u_made, 1)
                keep(2 * h, 2 * t + 2 * GS, False)
                act.wait_ge(centered, t + 1)
                nc.scalar.activation(sq, center_bank, ACT.Square).then_inc(squared, 1)
                keep(2 * h + 1, 2 * t + (2 * GS + 1), False)
                act.wait_ge(var_ps, t + 1)
                if not first:
                    act.wait_ge(inv_made, t)
                nc.scalar.activation(std, var_bank, ACT.Sqrt, bias=eps[:, 0:1]).then_inc(std_made, 1)

            pair_with_ln(0, 1, True)
            with act.Fori(0, GS // 2) as i:
                for h in range(2):
                    pair_with_ln(2 * i + (h + 1), h, False)
            for s in range(SLOTS):
                keep(s, NC - SLOTS + s, False)

            def keep_z(h, g, blocks):
                act.wait_ge(z_ps, g + 1)
                nc.scalar.activation(z_sb[:, h, 0:blocks], ps[:, h, 0:blocks * P].rearrange("p (b f) -> p b f", f=P), ACT.Copy
                                     ).then_inc(z_kept, 1)

            with act.Fori(0, NG // 2) as i:
                for h in range(2):
                    keep_z(h, 2 * i + h, GROUP)
            keep_z(0, NG, 1)

            def keep_sums(h, g, blocks):
                act.wait_ge(tabs_summed, g + 1)
                nc.scalar.activation(sums_T[:, h, 0:blocks], summed_T[h][:, 0:blocks], ACT.Copy).then_inc(tabs_kept, 1)

            def out_std(h, g, blocks):
                act.wait_ge(o_mv_made, g + 1)
                nc.scalar.activation(o_std[:, h, 0:blocks], o_mv[:, h, 0:blocks, 1], ACT.Sqrt, bias=eps[:, 0:1]).then_inc(o_std_made, 1)

            def norm(h, g, blocks, stores, count):
                act.wait_ge(o_shift_made, g + 1)
                if stores is not None:
                    act.wait_ge(stored[h], stores)
                for b in range(blocks):
                    last = nc.scalar.activation(normed[:, h, b], biased[:, h, b], ACT.Identity,
                                                scale=o_inv[:, h, b:b + 1], bias=o_shift[:, h, b:b + 1])
                last.then_inc(o_made, 1)
                act.wait_ge(o_made, g + 1)
                act.dma_start(out[bass.ds(g * (GROUP * P), count)].rearrange("(b p) f -> p b f", b=blocks),
                              normed[0:count // blocks, h, 0:blocks]).then_inc(stored[h], 16)

            def four_groups(i, first):
                keep_sums(0, SLOTS * i, GROUP)
                for s in range(SLOTS):
                    if s < SLOTS - 1:
                        keep_sums((s + 1) % 2, SLOTS * i + (s + 1), GROUP)
                    out_std(s % 2, SLOTS * i + s, GROUP)
                    norm(s % 2, SLOTS * i + s, GROUP, None if first and s < 2 else 32 * i + 16 * (s // 2), GROUP * P)

            four_groups(0, True)
            with act.Fori(1, NG // SLOTS) as i:
                four_groups(i, False)
            keep_sums(0, NG, 1)
            out_std(0, NG, 1)
            norm(0, NG, 1, 16 * (NG // 2), N - NG * GROUP * P)
            act.wait_ge(stored[0], 16 * (NG // 2 + 1))
            act.wait_ge(stored[1], 16 * (NG // 2))

        @block.vector
        def _(dve):
            v = nc.vector
            v.memset(ones[:], 1.0)
            v.memset(mean_w[:], 1.0 / P)
            v.memset(eps[:], EPS)
            dve.wait_ge(iotas_made, 1)
            v.tensor_copy(col[:], iota_i[:])
            v.tensor_copy(part[:], part_i[:]).then_inc(consts_made, 1)
            dve.wait_ge(consts_made, 1)
            v.tensor_scalar(ident[:], col[:], part[:, 0:1], None, ALU.is_equal)
            v.tensor_scalar(earlier[:], col[:], part[:, 0:1], None, ALU.is_lt)
            v.tensor_scalar(trash_row[:], part[:], float(TRASH), None, ALU.add).then_inc(consts_made, 1)
            dve.wait_ge(consts_made, 2)
            v.tensor_tensor(center[:], ident[:], mean_w[:], ALU.subtract).then_inc(consts_made, 1)

            dve.wait_ge(idx_loaded, 64)
            v.tensor_copy(src_rows, src_rows_i)
            v.tensor_copy(base_col, dst_rows_i[:, 0:1]).then_inc(rows_made, 1)
            v.tensor_scalar(mask_rows, mask_i, 0.0, None, ALU.is_lt).then_inc(rows_made, 1)
            dve.wait_ge(rows_made, 2)
            v.tensor_scalar(rel_rows, dst_rows_i, base_col, None, ALU.subtract)
            v.tensor_tensor(key_rows, number_i, src_rows, ALU.subtract).then_inc(rows_made, 1)
            dve.wait_ge(rows_turned, 1)
            for h in range(2):
                v.tensor_copy(gather_all[:, 0:NC, 4 * h:4 * h + 4].rearrange("p c j -> p j c"), turned[:, h]).then_inc(idx_kept, 1)
            dve.wait_ge(idx_kept, 2)
            for s in range(SLOTS):
                v.tensor_copy(gather_idx[:, s], gather_all[:, s]).then_inc(gather_idx_made, 1)
            dve.wait_ge(rows_made, 3)
            v.scalar_tensor_tensor(rel_rows, mask_rows, FAR, rel_rows, ALU.mult, ALU.add)
            v.tensor_tensor(key_rows, key_rows, mask_rows, ALU.mult).then_inc(rows_made, 1)
            dve.wait_ge(rows_made, 4)
            v.tensor_tensor(key_rows, key_rows, src_rows, ALU.add).then_inc(rows_made, 1)
            v.memset(dst_term[:, N:NPAD], 0.0)
            v.memset(key[:, NC:NC + 2], 0.0)
            v.memset(gather_all[:, NC:NC + SLOTS], 0)
            dve.wait_ge(rows_turned, 2)
            v.tensor_copy(base_i[:], base_ps)
            for a, kept in ((1, rel), (2, key)):
                for h in range(2):
                    last = v.tensor_copy(kept[:, 0:NC, 4 * h:4 * h + 4].rearrange("p c j -> p j c"), turned[:, 2 * a + h])
            last.then_inc(idx_made, 1)
            v.memset(acc_x[:], 0.0).then_inc(acc_x_zero, 1)

            dve.wait_ge(att_loaded, 16 * 3)
            v.tensor_scalar(diag[:, 0], ident[:], w_att_sb[:, 0:1], None, ALU.mult).then_inc(att_diag_made, 1)
            dve.wait_ge(att_spread, 1)
            v.tensor_copy(w_att_a[:], spread_ps[:, 0]).then_inc(att_kept, 1)

            dve.wait_ge(idx_made, 1)
            def src_products(s, product, o, done):
                for j in range(TPC):
                    last = v.tensor_tensor_reduce(product[:, j], rows[:, s, j, :], w_att_a[:], 1.0, 0.0, ALU.mult, ALU.add,
                                                  o[:, j:j + 1])
                last.then_inc(done, 1)

            def src_terms(s, i, c):
                dve.wait_ge(gathered[s], i * (16 * TPC) + 16 * TPC)
                v.tensor_copy(gather_idx[:, s], chunk_of(gather_all, c + SLOTS)).then_inc(gather_idx_made, 1)
                src_products(s, (same, dups)[s % 2], src_term[:, s % 2], src_term_made)

            def weigh(q, c):
                dve.wait_ge(att_made, c + 1)
                for j in range(TPC):
                    last = v.scalar_tensor_tensor(hot[:, q, j, :], col[:], rel[:, bass.ds(c, 1), j:j + 1].rearrange("p c j -> p (c j)"),
                                                  att[:, q, j, :], ALU.is_equal, ALU.mult)
                last.then_inc(hot_made, 1)

            def add_sums(q, c, first):
                node = dve.value_load(base_i[0:1, bass.ds(c, 1)], min_val=0, max_val=N - 1)
                dve.wait_ge(summed, c + 1)
                if not first:
                    dve.wait_ge(added, c)
                v.tensor_tensor(acc_x[:, bass.ds(node, P)], acc_x[:, bass.ds(node, P)], sum_ps[q], ALU.add)
                v.tensor_tensor(acc_w[:, bass.ds(node, P)], acc_w[:, bass.ds(node, P)], weight_ps[q], ALU.add).then_inc(added, 1)

            def first_loop(i, first):
                for s in range(SLOTS):
                    src_terms(s, i, SLOTS * i + s)
                    if s >= 1:
                        weigh((s - 1) % 2, SLOTS * i + s - 1)
                    if s >= 2:
                        add_sums(s % 2, SLOTS * i + s - 2, first and s == 2)
                weigh(1, SLOTS * i + 3)
                add_sums(0, SLOTS * i + 2, False)
                add_sums(1, SLOTS * i + 3, False)

            dve.wait_ge(att_kept, 1)
            dve.wait_ge(accs_zero, 1)
            dve.wait_ge(acc_x_zero, 1)
            first_loop(0, True)
            dve.wait_ge(w_loaded, 16 * N_W)
            v.tensor_tensor(b_gate[:], b_ih_sb[:, 0:2], b_hh_sb[:, 0:2], ALU.add)
            v.tensor_tensor(w_node_sb[:], w_node_sb[:], ident[:], ALU.add)
            v.tensor_scalar(diag[:, 1], ident[:], vecs[:, 3:4], None, ALU.mult).then_inc(weights_made, 1)
            v.tensor_scalar(left, rel[:], float(P), None, ALU.is_ge).then_inc(left_step, 1)
            dve.wait_ge(left_step, 1)
            v.scalar_tensor_tensor(left, rel[:], FAR / 2, left, ALU.is_lt, ALU.mult).then_inc(left_step, 1)
            dve.wait_ge(left_step, 2)
            v.scalar_tensor_tensor(left, rel[:], 0.0, left, ALU.is_lt, ALU.add).then_inc(left_step, 1)
            dve.wait_ge(left_step, 3)
            v.tensor_reduce(n_left[:], left, AX.XY, ALU.add).then_inc(left_step, 1)
            with dve.Fori(1, ITERS) as i:
                first_loop(i, False)
            dve.wait_ge(left_counted, 1)
            v.tensor_copy(n_left_i[:], ps[0:1, 6, 0:1]).then_inc(left_known, 1)

            def tiles(ap):
                return ap.unsqueeze(2).to_broadcast([P, TPC, P])

            def every(ap):
                return ap.unsqueeze(1).to_broadcast([P, TPC, P])

            dve.wait_ge(zeros_made, 2 * 16 * TABLES)

            dve.wait_ge(left_known, 1)
            with dve.If(dve.value_load(n_left_i[0:1, 0:1], min_val=0, max_val=E) > 0):
                dve.wait_ge(added, NC)
                v.tensor_copy(base_f, base_i[:]).then_inc(g_base, 1)
                dve.wait_ge(g_base_ps, 1)
                v.tensor_copy(base_bc, ps[:, 0, 0:NC]).then_inc(g_base, 1)
                dve.wait_ge(g_base, 2)
                with dve.Fori(0, NC) as c:
                    v.tensor_copy(gather_idx[:, 0], chunk_of(gather_all, c))
                    v.tensor_scalar(left_now, chunk_of(rel, c), base_bc[:, bass.ds(c, 1)], 1.0, ALU.add, ALU.add).then_inc(g_left, 1)
                    dve.wait_ge(g_left, 3 * c + 1)
                    v.tensor_tensor(left_now, left_now, chunk_of(left, c), ALU.mult).then_inc(g_left, 1)
                    dve.wait_ge(g_left, 3 * c + 2)
                    v.tensor_scalar(left_now, left_now, -1.0, None, ALU.add).then_inc(g_left, 1)
                    dve.wait_ge(g_left, 3 * c + 3)
                    v.tensor_copy(n_dups[:], left_now).then_inc(g_ready, 1)
                    dve.wait_ge(g_gathered, c * (16 * TPC) + 16 * TPC)
                    src_products(0, same, src_term[:, 0], g_src_term)
                    dve.wait_ge(g_src_term, c + 1)
                    dve.nop(nofuse=True)
                    with dve.Fori(0, NB) as b:
                        n = c * NB + b
                        v.tensor_tensor(hot[:, 0], every(col[:]), tiles(left_now), ALU.is_equal).then_inc(g_hot, 1)
                        dve.wait_ge(g_att, n + 1)
                        dve.wait_ge(g_hot, n + 1)
                        v.tensor_tensor(hot[:, 1], hot[:, 0], att[:, 0], ALU.mult)
                        v.tensor_scalar(left_now, left_now, -float(P), None, ALU.add).then_inc(g_weighted, 1)
                        dve.wait_ge(g_summed, n + 1)
                        for acc, bank in ((acc_x, sum_ps[0]), (acc_w, weight_ps[0]), (acc_in, sum_ps[1])):
                            last = v.tensor_tensor(acc[:, bass.ds(b * P, P)], acc[:, bass.ds(b * P, P)], bank, ALU.add)
                        last.then_inc(g_added, 1)
                        dve.wait_ge(g_added, n + 1)
            dve.wait_ge(added, NC)
            v.memset(n_dups[:], 0.0).then_inc(by_dst_done, 1)
            dve.wait_ge(by_dst_done, 1)

            def copy_keys(q, c):
                v.tensor_copy(key_now[:, q], chunk_of(key, c)).then_inc(keys_copied, 1)

            def find(q, s, c, first, second, first_quad):
                v.tensor_tensor(hot[:, q], every(col[:]), tiles(chunk_of(rel, c)), ALU.is_equal).then_inc(onehot_made, 1)
                if not first:
                    add_in(c - 1, second)
                dve.wait_ge(keys_spread, c + 1)
                if not first:
                    dve.wait_ge(merged, c)
                v.tensor_tensor(same[:], key_ps, tiles(chunk_of(key, c)), ALU.is_equal).then_inc(same_made, 1)
                dve.wait_ge(same_made, c + 1)
                v.tensor_tensor(dups[:], same[:], every(earlier[:]), ALU.mult).then_inc(dups_made, 1)
                copy_keys(q, c + 2)
                v.tensor_scalar(to_trash[:], chunk_of(key, c), -1.0, trash_row[:, 0:1], ALU.mult, ALU.add)
                dve.wait_ge(dups_made, c + 1)
                v.tensor_reduce(n_dups[:], dups[:], AX.X, ALU.add).then_inc(counted, 1)
                dve.wait_ge(counted, c + 1)
                v.scalar_tensor_tensor(moved[:], n_dups[:], 1.0, to_trash[:], ALU.min, ALU.mult).then_inc(moved_made, 1)
                dve.wait_ge(moved_made, c + 1)
                if not first_quad:
                    dve.wait_ge(scattered, c - 2)
                v.tensor_tensor(scatter_idx[:, s], moved[:], chunk_of(key, c), ALU.add).then_inc(scatter_idx_made, 1)

            def add_in(c, first):
                node = dve.value_load(base_i[0:1, bass.ds(c, 1)], min_val=0, max_val=N - 1)
                dve.wait_ge(in_summed, c + 1)
                if not first:
                    dve.wait_ge(in_added, c)
                v.tensor_tensor(acc_in[:, bass.ds(node, P)], acc_in[:, bass.ds(node, P)], in_ps, ALU.add
                                ).then_inc(in_added, 1)

            def pair(p, h, first, first_quad):
                find(0, 2 * h, 2 * p, first, False, first_quad)
                find(1, 2 * h + 1, 2 * p + 1, False, first, first_quad)

            def gru_pre(t):
                dve.wait_ge(reset_made, t + 1)
                v.scalar_tensor_tensor(tmp, new_h_bank, b_hh_sb[:, 2:3], reset, ALU.add, ALU.mult).then_inc(scaled, 1)
                dve.wait_ge(scaled, t + 1)
                v.tensor_tensor(pre, tmp, new_in_bank, ALU.add).then_inc(pre_made, 1)

            def gru_mix(t):
                nodes = bass.ds(t * GW, GW)
                dve.wait_ge(new_made, t + 1)
                v.tensor_tensor(tmp, xT_sb[:, nodes], new, ALU.subtract).then_inc(diff_made, 1)
                dve.wait_ge(diff_made, t + 1)
                dve.wait_ge(update_made, t + 1)
                v.tensor_tensor(tmp, tmp, update, ALU.mult).then_inc(mixed, 1)
                dve.wait_ge(mixed, t + 1)
                v.tensor_tensor(acc_x[:, nodes], tmp, new, ALU.add).then_inc(h_made, 1)
                dve.wait_ge(h_made, t + 1)
                v.bn_stats(stats[:, bass.ds(t * 6, 6)], acc_x[:, nodes]).then_inc(bn_stats_made, 1)

            copy_keys(0, 0)
            copy_keys(1, 1)
            def pair_with_gru(p, h, first_quad):
                find(0, 2 * h, 2 * p, False, False, first_quad)
                gru_pre(p - 1)
                find(1, 2 * h + 1, 2 * p + 1, False, False, first_quad)
                gru_mix(p - 1)

            pair(0, 0, True, True)
            pair_with_gru(1, 1, True)
            with dve.Fori(1, GS // 2) as i:
                for h in range(2):
                    pair_with_gru(2 * i + h, h, False)
            pair_with_gru(GS - 1, 0, False)
            gru_pre(GS - 1)
            gru_mix(GS - 1)

            dve.wait_ge(bn_stats_made, GS)
            v.bn_aggr(bn[:, 0:2], stats[:]).then_inc(bn_made[0], 1)
            dve.wait_ge(bn_made[1], 1)
            v.reciprocal(bn_inv, bn_std).then_inc(bn_made[2], 1)
            dve.wait_ge(bn_made[2], 1)
            v.tensor_tensor(bn_scale, bn_inv, vecs[:, 0:1], ALU.mult).then_inc(bn_made[3], 1)
            dve.wait_ge(bn_made[3], 1)
            v.tensor_tensor(bn_off, bn_mean, bn_scale, ALU.mult).then_inc(bn_made[4], 1)
            dve.wait_ge(bn_made[4], 1)
            v.tensor_tensor(bn_shift, vecs[:, 1:2], bn_off, ALU.subtract).then_inc(bn_made[5], 1)

            u, std, inv = agg, reset, tmp

            def pair_with_ln(t, h, first):
                nodes = bass.ds(t * GW, GW)
                dve.wait_ge(u_made, t + 1)
                if not first:
                    dve.wait_ge(centered, t)
                v.tensor_tensor(y, u, xT_sb[:, nodes], ALU.add).then_inc(y_made, 1)
                pair(t + GS, h, False, False)
                dve.wait_ge(std_made, t + 1)
                v.reciprocal(inv, std).then_inc(inv_made, 1)
                dve.wait_ge(inv_made, t + 1)
                v.tensor_tensor(acc_x[:, nodes], center_bank, inv, ALU.mult).then_inc(x1_made, 1)

            pair_with_ln(0, 1, True)
            with dve.Fori(0, GS // 2) as i:
                for h in range(2):
                    pair_with_ln(2 * i + (h + 1), h, False)
            for h in range(2):
                pair(2 * GS + h, h, False, False)
            add_in(NC - 1, False)

            dve.wait_ge(bias_spread, 1)
            v.tensor_copy(bias_all[:], spread_ps[:, 1]).then_inc(bias_kept, 1)
            dve.wait_ge(bias_kept, 1)

            def add_z(h, g, blocks):
                dve.wait_ge(z_turned, g + 1)
                v.tensor_tensor(by_node[:, bass.ds(g * GROUP, blocks)], turned_z[h][:, 0:blocks],
                                bias_all[:].unsqueeze(1).to_broadcast([P, blocks, P]), ALU.add).then_inc(z_added, 1)

            with dve.Fori(0, NG // 2) as i:
                for h in range(2):
                    add_z(h, 2 * i + h, GROUP)
            add_z(0, NG, 1)

            def moments(h, g, blocks, first):
                dve.wait_ge(out_ps, g + 1)
                dve.wait_ge(z_added, NG + 1)
                if not first:
                    dve.wait_ge(o_made, g - 1)
                v.tensor_tensor(biased[:, h, 0:blocks], out_bank[h][:, 0:blocks], by_node[:, bass.ds(g * GROUP, blocks)], ALU.add
                                ).then_inc(o_added, 1)
                dve.wait_ge(o_added, g + 1)
                for b in range(blocks):
                    last = v.bn_stats(o_stat[:, h, b], biased[:, h, b])
                last.then_inc(o_stats_made, 1)
                dve.wait_ge(o_stats_made, g + 1)
                dve.nop(nofuse=True)
                for b in range(blocks):
                    last = v.bn_aggr(o_mv[:, h, b], o_stat[:, h, b])
                last.then_inc(o_mv_made, 1)

            def scale_shift(h, g, blocks):
                dve.wait_ge(o_std_made, g + 1)
                v.reciprocal(o_inv[:, h, 0:blocks], o_std[:, h, 0:blocks]).then_inc(o_inv_made, 1)
                dve.wait_ge(o_inv_made, g + 1)
                v.scalar_tensor_tensor(o_shift[:, h, 0:blocks], o_mv[:, h, 0:blocks, 0], -1.0, o_inv[:, h, 0:blocks],
                                       ALU.mult, ALU.mult).then_inc(o_shift_made, 1)

            def four_groups(i, first):
                for s in range(SLOTS):
                    moments(s % 2, SLOTS * i + s, GROUP, first and s < 2)
                    scale_shift(s % 2, SLOTS * i + s, GROUP)

            four_groups(0, True)
            with dve.Fori(1, NG // SLOTS) as i:
                four_groups(i, False)
            moments(0, NG, 1, False)
            scale_shift(0, NG, 1)

        @block.tensor
        def _(pe):
            mm = nc.tensor.matmul

            def turn(a, by_chunk):
                tile = by_chunk.rearrange("c (p j) -> c j p", j=TPC)
                for j in range(TPC):
                    last = nc.tensor.transpose(turned[:, 2 * a + j // 4, j % 4], tile[:, j], ident[0:NC, 0:NC])
                return last

            pe.wait_ge(consts_made, 3)
            pe.wait_ge(rows_made, 1)
            turn(0, src_rows).then_inc(rows_turned, 1)
            pe.wait_ge(rows_made, 5)
            nc.tensor.transpose(base_ps, base_col, ident[0:NC, 0:NC])
            turn(1, rel_rows)
            turn(2, key_rows).then_inc(rows_turned, 1)

            pe.wait_ge(att_diag_made, 1)
            mm(spread_ps[:, 0], ones[:], diag[:, 0], start=True, stop=True).then_inc(att_spread, 1)

            pe.wait_ge(x_loaded, 16)
            pe.wait_ge(idx_made, 1)

            def dst_terms(q, t, width):
                mm(ps[:, q, 0:width], w_att_sb[:, 1:2].to_broadcast([P, P]), xT_sb[:, bass.ds(t * AW, width)],
                   start=True, stop=True).then_inc(dst_term_ps, 1)

            dst_terms(0, 0, AW)
            dst_terms(1, 1, AW)
            with pe.Fori(1, AS // 2) as i:
                for q in range(2):
                    pe.wait_ge(dst_term_sb, 2 * i + (q - 1))
                    dst_terms(q, 2 * i + q, AW)
            pe.wait_ge(dst_term_sb, AS - 1)
            dst_terms(0, AS, GW)
            pe.wait_ge(dst_term_sb, AS + 1)

            def window_sum(bank, values, weights):
                for j in range(TPC):
                    last = mm(bank, values(j), weights[:, j, :], start=(j == 0), stop=(j == TPC - 1))
                return last

            with pe.Fori(0, ITERS) as i:
                for s in range(SLOTS):
                    q = s % 2
                    pe.wait_ge(hot_made, SLOTS * i + s + 1)
                    window_sum(sum_ps[q], lambda j: rows[:, s, j, :], hot[:, q])
                    window_sum(weight_ps[q], lambda j: ones[:, 0:1], hot[:, q]).then_inc(summed, 1)

            pe.wait_ge(left_step, 4)
            mm(ps[0:1, 6, 0:1], n_left[:], ones[:, 0:1], start=True, stop=True).then_inc(left_counted, 1)
            pe.wait_ge(left_known, 1)
            with pe.If(pe.value_load(n_left_i[0:1, 0:1], min_val=0, max_val=E) > 0):
                pe.wait_ge(g_base, 1)
                mm(ps[:, 0, 0:NC], ones[0:1, :], base_f, start=True, stop=True).then_inc(g_base_ps, 1)
                with pe.Fori(0, NC) as c:
                    pe.wait_ge(g_loaded, 16 * c + 16)
                    pe.nop(nofuse=True)
                    with pe.Fori(0, NB) as b:
                        pe.wait_ge(g_weighted, c * NB + b + 1)
                        window_sum(sum_ps[0], lambda j: rows[:, 0, j, :], hot[:, 1])
                        window_sum(weight_ps[0], lambda j: ones[:, 0:1], hot[:, 1])
                        window_sum(sum_ps[1], lambda j: ea[:, 0, j, :], hot[:, 0]).then_inc(g_summed, 1)
            pe.wait_ge(by_dst_done, 1)

            def spread_keys(q, c):
                pe.wait_ge(keys_copied, c + 1)
                for j in range(TPC):
                    last = nc.tensor.transpose(key_ps[:, j], key_now[:, q, j:j + 1].to_broadcast([P, P]), ident[:])
                last.then_inc(keys_spread, 1)

            def chunk(q, i, first):
                c = 2 * i + q
                pe.wait_ge(ea_loaded[q], 16 * i + 16)
                pe.wait_ge(onehot_made, c + 1)
                if not first:
                    pe.wait_ge(in_added, c)
                window_sum(in_ps, lambda j: ea[:, q, j, :], hot[:, q]).then_inc(in_summed, 1)
                pe.wait_ge(same_made, c + 1)
                spread_keys(1 - q, c + 1)
                if not first:
                    pe.wait_ge(merged_kept, c)
                for j in range(TPC):
                    last = mm(merge_ps[:, j], same[:, j, :], ea[:, q, j, :], start=True, stop=True)
                last.then_inc(merged, 1)

            def gru_agg(t, first):
                nodes = bass.ds(t * GW, GW)
                if not first:
                    pe.wait_ge(reset_made, t)
                mm(agg_bank, w_msg_sb[:], acc_x[:, nodes], start=True, stop=False)
                mm(agg_bank, b_msg_row[:], acc_w[:, nodes], start=False, stop=True).then_inc(agg_ps, 1)

            def gru_gates(t, first):
                nodes = bass.ds(t * GW, GW)
                pe.wait_ge(agg_sb, t + 1)
                if not first:
                    pe.wait_ge(pre_made, t)
                    pe.wait_ge(update_made, t)
                for g, bank in enumerate((reset_bank, update_bank)):
                    mm(bank, w_ih_sb[:, g * P:(g + 1) * P], agg, start=True, stop=False)
                    mm(bank, w_hh_sb[:, g * P:(g + 1) * P], xT_sb[:, nodes], start=False, stop=True)
                mm(new_in_bank, w_ih_sb[:, 2 * P:], agg, start=True, stop=True)
                mm(new_h_bank, w_hh_sb[:, 2 * P:], xT_sb[:, nodes], start=True, stop=True).then_inc(gates_ps, 1)

            def pair_with_gru(i, first):
                chunk(0, i, first)
                gru_agg(i, first)
                chunk(1, i, False)
                gru_gates(i, first)

            pe.wait_ge(weights_made, 1)
            spread_keys(0, 0)
            pair_with_gru(0, True)
            with pe.Fori(1, GS) as i:
                pair_with_gru(i, False)

            def pair_with_ln(t, first):
                chunk(0, t + GS, False)
                pe.wait_ge(y_made, t + 1)
                if not first:
                    pe.wait_ge(x1_made, t)
                mm(center_bank, center[:], y, start=True, stop=True).then_inc(centered, 1)
                chunk(1, t + GS, False)
                pe.wait_ge(squared, t + 1)
                mm(var_bank, mean_w[:], sq, start=True, stop=True).then_inc(var_ps, 1)

            pe.wait_ge(pre_made, GS)
            pe.wait_ge(update_made, GS)
            pair_with_ln(0, True)
            with pe.Fori(1, GS) as t:
                pair_with_ln(t, False)
            with pe.Fori(2 * GS, PAIRS) as i:
                chunk(0, i, False)
                chunk(1, i, False)

            def project(h, g, blocks, first):
                nodes = bass.ds(g * (GROUP * P), blocks * P)
                if not first:
                    pe.wait_ge(z_kept, g - 1)
                mm(ps[:, h, 0:blocks * P], w_node_sb[:], acc_x[:, nodes], start=True, stop=False)
                mm(ps[:, h, 0:blocks * P], w_in_sb[:], acc_in[:, nodes], start=False, stop=True).then_inc(z_ps, 1)

            def turn_z(h, g, blocks, first):
                pe.wait_ge(z_kept, g + 1)
                if not first:
                    pe.wait_ge(z_added, g - 1)
                for b in range(blocks):
                    last = nc.tensor.transpose(turned_z[h][:, b], z_sb[:, h, b], ident[:])
                last.then_inc(z_turned, 1)

            pe.wait_ge(x1_made, GS)
            mm(spread_ps[:, 1], ones[:], diag[:, 1], start=True, stop=False)
            mm(spread_ps[:, 1], vecs[:, 2:3].to_broadcast([P, P]), w_glob_sb[:], start=False, stop=True).then_inc(bias_spread, 1)
            pe.wait_ge(in_added, NC)
            pe.wait_ge(same_made, NC)
            for i, loop in ((0, None), (1, NG // 2)):
                if loop is None:
                    project(0, 0, GROUP, True)
                    project(1, 1, GROUP, True)
                    turn_z(0, 0, GROUP, True)
                    turn_z(1, 1, GROUP, True)
                else:
                    with pe.Fori(1, loop) as i:
                        for step in (project, turn_z):
                            for h in range(2):
                                step(h, 2 * i + h, GROUP, False)
            project(0, NG, 1, False)
            turn_z(0, NG, 1, False)

            def sum_tables(s, g, blocks, first):
                pe.wait_ge(tabs_halved, g + 1)
                if not first:
                    pe.wait_ge(tabs_kept, g - 1)
                for b in range(blocks):
                    for k in range(2):
                        last = mm(summed_T[s % 2][:, b], tabs[s][:, k, b], ident[:], start=(k == 0), stop=(k == 1))
                last.then_inc(tabs_summed, 1)

            def project_sums(h, g, blocks, first):
                pe.wait_ge(tabs_kept, g + 1)
                if not first:
                    pe.wait_ge(o_added, g - 1)
                else:
                    pe.wait_ge(bias_kept, 1)
                for b in range(blocks):
                    last = mm(out_bank[h][:, b], sums_T[:, h, b], w_out_sb[:], start=True, stop=True)
                last.then_inc(out_ps, 1)

            def four_groups(i, first):
                sum_tables(0, SLOTS * i, GROUP, first)
                for s in range(SLOTS):
                    if s < SLOTS - 1:
                        sum_tables(s + 1, SLOTS * i + (s + 1), GROUP, first and s == 0)
                    project_sums(s % 2, SLOTS * i + s, GROUP, first and s < 2)

            four_groups(0, True)
            with pe.Fori(1, NG // SLOTS) as i:
                four_groups(i, False)
            sum_tables(0, NG, 1, False)
            project_sums(0, NG, 1, False)


def kernel(**inputs):
    import numpy as np
    import concourse.bacc as bacc
    from concourse.bass_utils import run_bass_kernel_spmd

    a = {k: np.asarray(v) for k, v in inputs.items()}
    order = {
        "x": a["x"], "xT": a["x"].T, "src": a["src"], "dst": a["dst"], "edge_attr": a["edge_attr_128"],
        "W_msg": a["L0_gnn_W_msg"], "b_msg": a["L0_gnn_b_msg"], "W_att": a["L0_gnn_W_att"], "b_att": a["L0_gnn_b_att"],
        "W_ihT": a["L0_gnn_W_ih"].T, "b_ih": a["L0_gnn_b_ih"], "W_hhT": a["L0_gnn_W_hh"].T, "b_hh": a["L0_gnn_b_hh"],
        "gamma": a["L0_gnn_gamma"], "beta": a["L0_gnn_beta"], "glob": a["L1_gnn_global_features"],
        "W_nodeT": a["L1_gnn_W_node"].T, "W_inT": a["L1_gnn_W_incoming"].T, "W_outT": a["L1_gnn_W_outgoing"].T,
        "W_globT": a["L1_gnn_W_global"].T, "bias": a["L1_gnn_bias"],
    }
    nc = bacc.Bacc("TRN2", target_bir_lowering=False, num_devices=1)
    arrays, args = {}, []
    for name, v in order.items():
        v = np.ascontiguousarray(v)
        arrays[f"in_{name}"] = v
        args.append(nc.dram_tensor(f"in_{name}", v.shape, mybir.dt.from_np(v.dtype), kind="ExternalInput").ap())
    args.append(nc.dram_tensor("out_x", a["x"].shape, F32, kind="ExternalOutput").ap())
    gnn_two_layers(nc, *args)
    r = run_bass_kernel_spmd(nc, [arrays], core_ids=[0])
    return r.results[0]["out_x"]
```

```python
from contextlib import ExitStack

import concourse.bass as bass
from concourse import mybir

ALU = mybir.AluOpType
ACT = mybir.ActivationFunctionType
AX = mybir.AxisListType
F32 = mybir.dt.float32
I32 = mybir.dt.int32
U32 = mybir.dt.uint32

P = 128
TPC = 8
CHUNK = P * TPC
SLOTS = 4
GROUP = 4
TABLES = 4
BANK = 512
GW = 250
AW = 500
EPS = 1e-5
FAR = 20000.0


def gnn_two_layers(nc, x, xT, src, dst, edge_attr, W_msg, b_msg, W_att, b_att, W_ihT, b_ih, W_hhT, b_hh,
                   gamma, beta, glob, W_nodeT, W_inT, W_outT, W_globT, bias, out):
    N = x.shape[0]
    E = edge_attr.shape[0]
    NC = -(-E // CHUNK)
    WHOLE = NC - 1
    LAST = E - CHUNK
    DONE = WHOLE * CHUNK - LAST
    NB = -(-N // P)
    NPAD = (NB + 1) * P
    TRASH = NB * P
    MASKED = TRASH + P
    ROWS = MASKED + 2 * P
    GS = N // GW
    PAIRS = NC // 2
    AS = N // AW
    ITERS = NC // SLOTS
    MID = ITERS // 2
    STOPS = (MID, MID + ITERS // 6, MID + 2 * (ITERS // 6), ITERS)
    assert NC % SLOTS == 0 and N % GW == 0 and GS % 2 == 1 and NC <= P and DONE <= 2 * P
    NG = NB // GROUP
    assert N - AS * AW == GW and AS % 4 == 0 and ROWS % P == 0 and NB % GROUP == 1 and NG % SLOTS == 0
    assert NC % 4 == 0 and 2 * GS + 2 == PAIRS and TABLES == 4

    with ExitStack() as ctx:
        def sb(name, shape, dt=F32):
            return ctx.enter_context(nc.sbuf_tensor(name, shape, dt))

        def sem(name):
            return ctx.enter_context(nc.semaphore(name))

        ps = ctx.enter_context(nc.psum_tensor("ps", [P, 8, BANK], F32))

        tables = [nc.dram_tensor(f"by_src_{k}", [ROWS, P], F32, kind="Internal").ap() for k in range(TABLES)]

        iota_i = sb("iota_i", [P, P], I32)
        part_i = sb("part_i", [P, 1], I32)
        col = sb("col", [P, P])
        part = sb("part", [P, 1])
        trash_row = sb("trash_row", [P, 1])
        ident = sb("ident", [P, P])
        earlier = sb("earlier", [P, P])
        ones = sb("ones", [P, P])
        mean_w = sb("mean_w", [P, P])
        center = sb("center", [P, P])
        eps = sb("eps", [P, 1])

        base_i = sb("base_i", [1, NC], I32)
        gather_all = sb("gather_all", [P, NC + SLOTS, TPC], U32)
        rel = sb("rel", [P, NC, TPC])
        key = sb("key", [P, NC + 2, TPC])
        key_now = sb("key_now", [P, 2, TPC])
        n_left = sb("n_left", [P, 1])
        n_left_i = sb("n_left_i", [1, 1], I32)
        gather_idx = sb("gather_idx", [P, SLOTS, TPC], U32)
        scatter_idx = sb("scatter_idx", [P, SLOTS, TPC], U32)

        xT_sb = sb("xT_sb", [P, NB * P])
        by_node = xT_sb[:].rearrange("p (b f) -> p b f", f=P)
        w_att_sb = sb("w_att_sb", [P, 2])
        diag = sb("diag", [P, 2, P])
        w_att_a = sb("w_att_a", [P, P])
        b_att_sb = sb("b_att_sb", [P, 1])
        w_msg_sb = sb("w_msg_sb", [P, P])
        b_msg_row = sb("b_msg_row", [1, P])
        w_ih_sb = sb("w_ih_sb", [P, 3 * P])
        w_hh_sb = sb("w_hh_sb", [P, 3 * P])
        b_ih_sb = sb("b_ih_sb", [P, 3])
        b_hh_sb = sb("b_hh_sb", [P, 3])
        b_gate = sb("b_gate", [P, 2])
        vecs = sb("vecs", [P, 4])
        w_glob_sb = sb("w_glob_sb", [P, P])
        w_node_sb = sb("w_node_sb", [P, P])
        w_in_sb = sb("w_in_sb", [P, P])
        w_out_sb = sb("w_out_sb", [P, P])
        bias_all = sb("bias_all", [P, P])

        dst_term = sb("dst_term", [P, NPAD])
        acc_x = sb("acc_x", [P, NPAD])
        acc_w = sb("acc_w", [1, NPAD])
        acc_in = sb("acc_in", [P, NPAD])

        rows = sb("rows", [P, SLOTS, TPC, P])
        ea = sb("ea", [P, 2, TPC, P])
        src_term = sb("src_term", [P, 2, TPC])
        att = sb("att", [P, SLOTS, TPC, P])
        hot = sb("hot", [P, 2, TPC, P])
        same = sb("same", [P, TPC, P])
        dups = sb("dups", [P, TPC, P])
        n_dups = sb("n_dups", [P, TPC])
        moved = sb("moved", [P, TPC])
        to_trash = sb("to_trash", [P, TPC])
        stats = sb("stats", [P, GS * 6])
        bn = sb("bn", [P, 7])
        bn_mean, bn_var, bn_std, bn_inv, bn_scale, bn_off, bn_shift = (bn[:, k:k + 1] for k in range(7))

        src_rows, rel_rows, key_rows, mask_rows = (acc_x[0:NC, k * CHUNK:(k + 1) * CHUNK] for k in range(4))
        hot_c = hot[0:NC].rearrange("c s j f -> c s (j f)")
        src_rows_i, dst_rows_i = (hot_c[:, s].bitcast(I32) for s in range(2))
        att_c = att[0:NC].rearrange("c s j f -> c s (j f)")
        mask_i, number_i = (att_c[:, s].bitcast(I32) for s in range(2))
        base_col = n_dups[0:NC, 0:1]

        agg, reset, update, new, pre, tmp, sq, y = (dst_term[:, k * GW:(k + 1) * GW] for k in range(8))
        D = 8 * GW
        z_sb, sums_T, biased, normed = (
            dst_term[:, D + k * 2 * BANK:D + (k + 1) * 2 * BANK].rearrange("p (h b f) -> p h b f", h=2, f=P) for k in range(4))
        o_stat = hot[:, 0, 0, 0:2 * GROUP * 6].rearrange("p (h b k) -> p h b k", h=2, k=6)
        o_mv = hot[:, 0, 1, 0:2 * GROUP * 2].rearrange("p (h b k) -> p h b k", h=2, k=2)
        o_std, o_inv, o_shift = (hot[:, 0, 2 + k, 0:2 * GROUP].rearrange("p (h b) -> p h b", h=2) for k in range(3))
        tabs = [buf[:, 2 * h:2 * h + 2].rearrange("p s j f -> p (s j) f").rearrange("p (k b) f -> p k b f", k=TABLES)
                for buf in (rows, att) for h in range(2)]
        base_bc = dups[:, 0, 0:NC]
        base_f = dups[0:1, 1, 0:NC]
        left_now = moved[:]
        left = ea[:, 1].rearrange("p j f -> p (j f)")[:, 0:NC * TPC].rearrange("p (c j) -> p c j", j=TPC)

        att_loaded = sem("att_loaded")
        iotas_made, consts_made = sem("iotas_made"), sem("consts_made")
        idx_loaded, w_loaded, x_loaded = sem("idx_loaded"), sem("w_loaded"), sem("x_loaded")
        first_idx_loaded = sem("first_idx_loaded")
        idx_kept, acc_x_zero = sem("idx_kept"), sem("acc_x_zero")
        rows_made, rows_turned, idx_made = sem("rows_made"), sem("rows_turned"), sem("idx_made")
        att_diag_made, att_spread, att_kept, weights_made, bias_spread, bias_kept = (
            sem(n) for n in ("att_diag_made", "att_spread", "att_kept", "weights_made", "bias_spread", "bias_kept"))
        dst_term_ps, dst_term_sb, accs_zero = sem("dst_term_ps"), sem("dst_term_sb"), sem("accs_zero")
        left_step, left_counted, left_known = sem("left_step"), sem("left_counted"), sem("left_known")
        gather_idx_made = sem("gather_idx_made")
        gathered = [sem(f"gathered{s}") for s in range(SLOTS)]
        src_term_made, att_made, hot_made = sem("src_term_made"), sem("att_made"), sem("hot_made")
        summed, added = sem("summed"), sem("added")
        g_base, g_base_ps, g_left, g_ready, g_loaded, g_gathered = (
            sem(n) for n in ("g_base", "g_base_ps", "g_left", "g_ready", "g_loaded", "g_gathered"))
        g_src_term, g_hot, g_att, g_weighted, g_summed, g_added = (
            sem(n) for n in ("g_src_term", "g_hot", "g_att", "g_weighted", "g_summed", "g_added"))
        general_done, by_dst_done, rows_used = sem("general_done"), sem("by_dst_done"), sem("rows_used")
        zeros_made = sem("zeros_made")
        table_free = [sem(f"table_free{k}") for k in range(TABLES)]
        ea_loaded = [sem(f"ea_loaded{q}") for q in range(2)]
        keys_copied, keys_spread, onehot_made, same_made, dups_made = (
            sem(n) for n in ("keys_copied", "keys_spread", "onehot_made", "same_made", "dups_made"))
        counted, moved_made, scatter_idx_made = sem("counted"), sem("moved_made"), sem("scatter_idx_made")
        in_summed, in_added, merged, merged_kept = (
            sem("in_summed"), sem("in_added"), sem("merged"), sem("merged_kept"))
        scattered = sem("scattered")
        agg_ps, agg_sb, gates_ps, reset_made, update_made, scaled, pre_made, new_made, diff_made, mixed, h_made, bn_stats_made = (
            sem(n) for n in ("agg_ps", "agg_sb", "gates_ps", "reset_made", "update_made", "scaled", "pre_made", "new_made",
                             "diff_made", "mixed", "h_made", "bn_stats_made"))
        bn_made = [sem(f"bn_made{k}") for k in range(7)]
        u_made, y_made, centered, squared, var_ps, std_made, inv_made, x1_made = (
            sem(n) for n in ("u_made", "y_made", "centered", "squared", "var_ps", "std_made", "inv_made", "x1_made"))
        tabs_loaded = [sem(f"tabs_loaded{s}") for s in range(SLOTS)]
        z_ps, z_kept, z_turned, z_added = (sem(n) for n in ("z_ps", "z_kept", "z_turned", "z_added"))
        tabs_halved, tabs_summed, tabs_kept, out_ps = (
            sem(n) for n in ("tabs_halved", "tabs_summed", "tabs_kept", "out_ps"))
        o_added, o_stats_made, o_mv_made, o_std_made, o_inv_made, o_shift_made, o_made = (
            sem(n) for n in ("o_added", "o_stats_made", "o_mv_made", "o_std_made", "o_inv_made", "o_shift_made", "o_made"))
        stored = [sem(f"stored{h}") for h in range(2)]

        turned = ps[:, 0:6, 0:4 * NC].rearrange("p b (j c) -> p b j c", c=NC)
        base_ps = ps[0:1, 6, 0:NC]
        spread_ps = ps[:, 7, 0:2 * P].rearrange("p (v f) -> p v f", v=2)
        sum_ps = [ps[:, 5 + q, 0:P] for q in range(2)]
        weight_ps = [ps[0:1, 5 + q, P:2 * P] for q in range(2)]
        left_ps, base_bc_ps = ps[0:1, 7, 0:1], ps[:, 7, 0:NC]
        key_ps = ps[:, 0:2].rearrange("p b (j f) -> p (b j) f", f=P)
        in_ps = ps[:, 2, 0:P]
        merge_ps = ps[:, 3:5].rearrange("p b (j f) -> p (b j) f", f=P)
        agg_bank, reset_bank, update_bank = ps[:, 5, 0:GW], ps[:, 5, GW:2 * GW], ps[:, 6, 0:GW]
        new_in_bank, new_h_bank = ps[:, 7, 0:GW], ps[:, 7, GW:2 * GW]
        center_bank, var_bank = ps[:, 5, 0:GW], ps[:, 6, 0:GW]

        turned_z = [ps[:, 2 + h].rearrange("p (b f) -> p b f", f=P) for h in range(2)]
        summed_T = [ps[:, 4 + h].rearrange("p (b f) -> p b f", f=P) for h in range(2)]
        out_bank = [ps[:, 6 + h].rearrange("p (b f) -> p b f", f=P) for h in range(2)]

        def chunk_of(array, c):
            return array[:, bass.ds(c, 1)].rearrange("p c j -> p (c j)")

        block = ctx.enter_context(nc.Block())
        N_W = 18

        @block.sync
        def _(sp):
            sp.dma_start(gather_idx[:].bitcast(I32), src[0:SLOTS * CHUNK].rearrange("(c p j) -> p c j", p=P, j=TPC)
                         ).then_inc(first_idx_loaded, 16)
            sp.dma_start(src_rows_i[0:WHOLE], src[0:WHOLE * CHUNK].rearrange("(c e) -> c e", e=CHUNK)).then_inc(idx_loaded, 16)
            sp.dma_start(dst_rows_i[0:WHOLE], dst[0:WHOLE * CHUNK].rearrange("(c e) -> c e", e=CHUNK)).then_inc(idx_loaded, 16)
            sp.dma_start(src_rows_i[WHOLE:NC], src[LAST:E].rearrange("(c e) -> c e", c=1)).then_inc(idx_loaded, 16)
            sp.dma_start(dst_rows_i[WHOLE:NC], dst[LAST:E].rearrange("(c e) -> c e", c=1)).then_inc(idx_loaded, 16)
            sp.dma_start(xT_sb[:, 0:N], xT).then_inc(x_loaded, 16)

            def column(a):
                return a.rearrange("(p o) -> p o", o=1)

            for o, a in ((w_msg_sb[:], W_msg), (b_msg_row[:], b_msg.rearrange("(o d) -> o d", o=1)),
                         (w_ih_sb[:], W_ihT), (w_hh_sb[:], W_hhT),
                         (vecs[:, 0:1], column(gamma)), (vecs[:, 1:2], column(beta)),
                         (vecs[:, 2:3], column(glob[0])), (vecs[:, 3:4], column(bias)),
                         (w_glob_sb[:], W_globT), (w_node_sb[:], W_nodeT), (w_in_sb[:], W_inT), (w_out_sb[:], W_outT),
                         *[(b_ih_sb[:, g:g + 1], column(b_ih[g * P:(g + 1) * P])) for g in range(3)],
                         *[(b_hh_sb[:, g:g + 1], column(b_hh[g * P:(g + 1) * P])) for g in range(3)]):
                sp.dma_start(o, a).then_inc(w_loaded, 16)

            def edges_from(first_edge):
                return edge_attr[bass.ds(first_edge, CHUNK)].rearrange("(p j) f -> p j f", j=TPC)

            sp.wait_ge(accs_zero, 1)
            for k in range(TABLES):
                sp.wait_ge(hot_made, (k + 1) * (SLOTS * MID // (TABLES + 1)))
                flat = tables[k].rearrange("(p a) f -> p (a f)", p=P)
                sp.dma_start(flat[:, 0:NPAD], acc_in[:]).then_inc(zeros_made, 16)
                sp.dma_start(flat[:, NPAD:ROWS], acc_in[:, 0:ROWS - NPAD]).then_inc(zeros_made, 16)

            sp.wait_ge(left_known, 1)
            with sp.If(sp.value_load(n_left_i[0:1, 0:1], min_val=0, max_val=E) > 0):
                with sp.Fori(0, WHOLE) as c:
                    sp.wait_ge(g_ready, c + 1)
                    sp.dma_start(ea[:, 0], edges_from(c * CHUNK)).then_inc(g_loaded, 16)
                sp.wait_ge(g_ready, NC)
                sp.dma_start(ea[:, 0], edges_from(LAST)).then_inc(g_loaded, 16)
                sp.wait_ge(g_added, NC * NB)

            def load(q, c, first_edge):
                sp.dma_start(ea[:, q], edges_from(first_edge)).then_inc(ea_loaded[q], 16)

            load(0, 0, 0)
            sp.wait_ge(general_done, 1)
            load(1, 1, CHUNK)
            with sp.Fori(1, PAIRS - 1) as i:
                for q in range(2):
                    sp.wait_ge(merged, 2 * i + (q - 1))
                    load(q, 2 * i + q, i * (2 * CHUNK) + q * CHUNK)
            sp.wait_ge(merged, NC - 3)
            load(0, NC - 2, (NC - 2) * CHUNK)
            sp.wait_ge(merged, NC - 2)
            load(1, NC - 1, LAST)

            def load_tables(s, g, blocks):
                for k in range(TABLES):
                    sp.dma_start(tabs[s][:, k, 0:blocks],
                                 tables[k][bass.ds(g * (GROUP * P), blocks * P)].rearrange("(b p) f -> p b f", p=P)
                                 ).then_inc(tabs_loaded[s], 16)

            for k in range(TABLES):
                sp.wait_ge(table_free[k], 16 * (NC * TPC // TABLES))
            for s in range(SLOTS):
                load_tables(s, s, GROUP)
            with sp.Fori(1, NG // SLOTS) as i:
                for s in range(SLOTS):
                    sp.wait_ge(tabs_summed, SLOTS * i + (s + 1 - SLOTS))
                    load_tables(s, i * SLOTS + s, GROUP)
            sp.wait_ge(tabs_summed, NG + 1 - SLOTS)
            load_tables(0, NG, 1)

        @block.gpsimd
        def _(pool):
            nc.gpsimd.iota(iota_i[:], [[1, P]], base=0, channel_multiplier=0)
            nc.gpsimd.iota(part_i[:], [[1, 1]], base=0, channel_multiplier=1)
            nc.gpsimd.iota(mask_i, [[1, CHUNK]], base=WHOLE * CHUNK - DONE, channel_multiplier=-CHUNK)
            nc.gpsimd.iota(number_i, [[1, CHUNK]], base=MASKED, channel_multiplier=0).then_inc(iotas_made, 1)

            def gather(idx, s, done):
                for j in range(TPC):
                    pool.indirect_dma_start(rows[:, s, j, :], None, x,
                                            bass.IndirectOffsetOnAxis(ap=idx[:, s, j:j + 1], axis=0)
                                            ).then_inc(done, 16)

            pool.wait_ge(first_idx_loaded, 16)
            for s in range(SLOTS):
                gather(gather_idx, s, gathered[s])

            def gather_four(i):
                for s in range(SLOTS):
                    pool.wait_ge(rows_used, SLOTS * i + (s + 1 - SLOTS))
                    pool.nop(nofuse=True)
                    pool.wait_ge(gather_idx_made, SLOTS * i + (s + 1 - SLOTS))
                    pool.nop(nofuse=True)
                    gather(gather_idx, s, gathered[s])

            with pool.Fori(1, MID) as i:
                gather_four(i)

            pool.wait_ge(left_known, 1)
            with pool.If(pool.value_load(n_left_i[0:1, 0:1], min_val=0, max_val=E) > 0):
                with pool.Fori(0, NC) as c:
                    pool.wait_ge(g_ready, c + 1)
                    pool.nop(nofuse=True)
                    gather(scatter_idx, 0, g_gathered)
                pool.wait_ge(g_summed, NC * NB)
            with pool.Fori(MID, ITERS) as i:
                gather_four(i)

            pool.wait_ge(zeros_made, 2 * 16 * TABLES)

            def scatter(s, c, first):
                pool.wait_ge(scatter_idx_made, c + 1)
                pool.nop(nofuse=True)
                pool.wait_ge(merged_kept, c + 1)
                pool.nop(nofuse=True)
                for j in range(TPC):
                    k, turn = j % TABLES, j // TABLES
                    if not (first and turn == 0):
                        pool.wait_ge(table_free[k], c * (16 * TPC // TABLES) + 16 * turn)
                        pool.nop(nofuse=True)
                    pool.indirect_dma_start(tables[k], bass.IndirectOffsetOnAxis(ap=scatter_idx[:, s, j:j + 1], axis=0),
                                            att[:, s, j, :], None, compute_op=ALU.add).then_inc(table_free[k], 16)
                    if j == TABLES - 1:
                        pool.sem_inc(scattered, 1)

            for k in range(SLOTS):
                scatter((k + 2) % SLOTS, k, k == 0)
            with pool.Fori(1, ITERS) as i:
                for k in range(SLOTS):
                    scatter((k + 2) % SLOTS, SLOTS * i + k, False)

            def halve(s, i, g, blocks):
                pool.wait_ge(tabs_loaded[s], i * (16 * TABLES) + 16 * TABLES)
                nc.gpsimd.tensor_tensor(tabs[s][:, 0:2, 0:blocks], tabs[s][:, 0:2, 0:blocks], tabs[s][:, 2:4, 0:blocks], ALU.add
                                        ).then_inc(tabs_halved, 1)

            with pool.Fori(0, NG // SLOTS) as i:
                for s in range(SLOTS):
                    halve(s, i, SLOTS * i + s, GROUP)
            halve(0, NG // SLOTS, NG, 1)

        @block.scalar
        def _(act):
            for o, a in ((w_att_sb[:, 0:1], W_att[0:P]), (w_att_sb[:, 1:2], W_att[P:2 * P]),
                         (b_att_sb[:], b_att.rearrange("(o d) -> o d", o=1).to_broadcast([P, 1]))):
                act.dma_start(o, a).then_inc(att_loaded, 16)

            act.wait_ge(consts_made, 1)
            nc.scalar.activation(acc_w[:], ones[0:1, 0:1].to_broadcast([1, NPAD]), ACT.Copy, scale=0.0)
            nc.scalar.activation(acc_in[:], ones[:, 0:1].to_broadcast([P, NPAD]), ACT.Copy, scale=0.0).then_inc(accs_zero, 1)

            act.wait_ge(att_loaded, 16 * 3)

            def keep_dst_term(q, t, width):
                act.wait_ge(dst_term_ps, t + 1)
                nc.scalar.activation(dst_term[:, bass.ds(t * AW, width)], ps[:, q, 0:width], ACT.Identity,
                                     bias=b_att_sb[:, 0:1]).then_inc(dst_term_sb, 1)

            with act.Fori(0, AS // 4) as i:
                for q in range(4):
                    keep_dst_term(q % 2, 4 * i + q, AW)
            keep_dst_term(0, AS, GW)

            def weights(q, src_terms, first_node, done):
                for j in range(TPC):
                    last = nc.scalar.activation(att[:, q, j, :], dst_term[:, bass.ds(first_node, P)], ACT.Sigmoid,
                                                bias=src_terms[:, j:j + 1])
                last.then_inc(done, 1)

            act.wait_ge(idx_made, 1)
            act.wait_ge(dst_term_sb, AS + 1)

            def weights_of_pairs(first, end):
                with act.Fori(first, end) as i:
                    for q in range(2):
                        c = 2 * i + q
                        node = act.value_load(base_i[0:1, bass.ds(c, 1)], min_val=0, max_val=N - 1)
                        act.wait_ge(src_term_made, c + 1)
                        weights(q, src_term[:, q], node, att_made)

            weights_of_pairs(0, MID * SLOTS // 2)

            act.wait_ge(left_known, 1)
            with act.If(act.value_load(n_left_i[0:1, 0:1], min_val=0, max_val=E) > 0):
                with act.Fori(0, NC) as c:
                    with act.Fori(0, NB) as b:
                        act.wait_ge(g_hot, c * NB + b + 1)
                        weights(0, src_term[:, 0], b * P, g_att)

            def keep(s, c, first_quad):
                if not first_quad:
                    act.wait_ge(scattered, c - 2)
                act.wait_ge(merged, c + 1)
                for h in range(2):
                    last = nc.scalar.activation(att[:, s, 4 * h:4 * h + 4, :], merge_ps[:, 4 * h:4 * h + 4, :], ACT.Copy)
                last.then_inc(merged_kept, 1)

            for c in range(3):
                if c < 2:
                    keep(c + 2, c, True)
                weights_of_pairs(STOPS[c] * SLOTS // 2, STOPS[c + 1] * SLOTS // 2)
            act.wait_ge(hot_made, NC)
            keep(0, 2, True)
            keep(1, 3, True)
            act.wait_ge(by_dst_done, 1)

            def gru_head(t):
                act.wait_ge(agg_ps, t + 1)
                nc.scalar.activation(agg, agg_bank, ACT.Copy).then_inc(agg_sb, 1)

            def gru_gates(t, first):
                act.wait_ge(gates_ps, t + 1)
                if not first:
                    act.wait_ge(h_made, t)
                nc.scalar.activation(reset, reset_bank, ACT.Sigmoid, bias=b_gate[:, 0:1]).then_inc(reset_made, 1)
                nc.scalar.activation(update, update_bank, ACT.Sigmoid, bias=b_gate[:, 1:2]).then_inc(update_made, 1)

            def gru_new(t):
                act.wait_ge(pre_made, t + 1)
                nc.scalar.activation(new, pre, ACT.Tanh, bias=b_ih_sb[:, 2:3]).then_inc(new_made, 1)

            def pair_with_gru(p, h, first):
                gru_gates(p - 2, first)
                keep(2 * h, 2 * p, False)
                gru_new(p - 2)
                gru_head(p - 1)
                keep(2 * h + 1, 2 * p + 1, False)

            act.wait_ge(weights_made, 1)
            gru_head(0)
            pair_with_gru(2, 1, True)
            pair_with_gru(3, 0, False)
            with act.Fori(2, (GS + 1) // 2) as i:
                for h in range(2):
                    pair_with_gru(2 * i + h, 1 - h, False)
            gru_gates(GS - 1, False)
            gru_new(GS - 1)

            act.wait_ge(bn_made[0], 1)
            nc.scalar.activation(bn_std, bn_var, ACT.Sqrt, bias=eps[:, 0:1]).then_inc(bn_made[1], 1)
            act.wait_ge(bn_made[5], 1)

            u, std = agg, reset

            def pair_with_ln(t, h, first):
                if not first:
                    act.wait_ge(y_made, t)
                nc.scalar.activation(u, acc_x[:, bass.ds(t * GW, GW)], ACT.Identity, scale=bn_scale, bias=bn_shift
                                     ).then_inc(u_made, 1)
                keep(2 * h, 2 * t + (2 * GS + 2), False)
                act.wait_ge(centered, t + 1)
                nc.scalar.activation(sq, center_bank, ACT.Square).then_inc(squared, 1)
                keep(2 * h + 1, 2 * t + (2 * GS + 3), False)
                act.wait_ge(var_ps, t + 1)
                if not first:
                    act.wait_ge(inv_made, t)
                nc.scalar.activation(std, var_bank, ACT.Sqrt, bias=eps[:, 0:1]).then_inc(std_made, 1)

            pair_with_ln(0, 1, True)
            with act.Fori(0, GS // 2) as i:
                for h in range(2):
                    pair_with_ln(2 * i + (h + 1), h, False)
            keep(0, NC - 2, False)
            keep(1, NC - 1, False)

            def keep_z(h, g, blocks):
                act.wait_ge(z_ps, g + 1)
                nc.scalar.activation(z_sb[:, h, 0:blocks], ps[:, h, 0:blocks * P].rearrange("p (b f) -> p b f", f=P), ACT.Copy
                                     ).then_inc(z_kept, 1)

            with act.Fori(0, NG // 2) as i:
                for h in range(2):
                    keep_z(h, 2 * i + h, GROUP)
            keep_z(0, NG, 1)

            def keep_sums(h, g, blocks):
                act.wait_ge(tabs_summed, g + 1)
                nc.scalar.activation(sums_T[:, h, 0:blocks], summed_T[h][:, 0:blocks], ACT.Copy).then_inc(tabs_kept, 1)

            def out_std(h, g, blocks):
                act.wait_ge(o_mv_made, g + 1)
                nc.scalar.activation(o_std[:, h, 0:blocks], o_mv[:, h, 0:blocks, 1], ACT.Sqrt, bias=eps[:, 0:1]).then_inc(o_std_made, 1)

            def norm(h, g, blocks, stores, count):
                act.wait_ge(o_shift_made, g + 1)
                if stores is not None:
                    act.wait_ge(stored[h], stores)
                for b in range(blocks):
                    last = nc.scalar.activation(normed[:, h, b], biased[:, h, b], ACT.Identity,
                                                scale=o_inv[:, h, b:b + 1], bias=o_shift[:, h, b:b + 1])
                last.then_inc(o_made, 1)
                act.wait_ge(o_made, g + 1)
                act.dma_start(out[bass.ds(g * (GROUP * P), count)].rearrange("(b p) f -> p b f", b=blocks),
                              normed[0:count // blocks, h, 0:blocks]).then_inc(stored[h], 16)

            def four_groups(i, first):
                keep_sums(0, SLOTS * i, GROUP)
                for s in range(SLOTS):
                    if s < SLOTS - 1:
                        keep_sums((s + 1) % 2, SLOTS * i + (s + 1), GROUP)
                    out_std(s % 2, SLOTS * i + s, GROUP)
                    norm(s % 2, SLOTS * i + s, GROUP, None if first and s < 2 else 32 * i + 16 * (s // 2), GROUP * P)

            four_groups(0, True)
            with act.Fori(1, NG // SLOTS) as i:
                four_groups(i, False)
            keep_sums(0, NG, 1)
            out_std(0, NG, 1)
            norm(0, NG, 1, 16 * (NG // 2), N - NG * GROUP * P)
            act.wait_ge(stored[0], 16 * (NG // 2 + 1))
            act.wait_ge(stored[1], 16 * (NG // 2))

        @block.vector
        def _(dve):
            v = nc.vector
            v.memset(ones[:], 1.0)
            v.memset(mean_w[:], 1.0 / P)
            v.memset(eps[:], EPS)
            dve.wait_ge(iotas_made, 1)
            v.tensor_copy(col[:], iota_i[:])
            v.tensor_copy(part[:], part_i[:]).then_inc(consts_made, 1)
            dve.wait_ge(consts_made, 1)
            v.tensor_scalar(ident[:], col[:], part[:, 0:1], None, ALU.is_equal)
            v.tensor_scalar(earlier[:], col[:], part[:, 0:1], None, ALU.is_lt)
            v.tensor_scalar(trash_row[:], part[:], float(TRASH), None, ALU.add).then_inc(consts_made, 1)
            dve.wait_ge(consts_made, 2)
            v.tensor_tensor(center[:], ident[:], mean_w[:], ALU.subtract).then_inc(consts_made, 1)

            dve.wait_ge(att_loaded, 16 * 3)
            v.tensor_scalar(diag[:, 0], ident[:], w_att_sb[:, 0:1], None, ALU.mult).then_inc(att_diag_made, 1)
            dve.wait_ge(att_spread, 1)
            v.tensor_copy(w_att_a[:], spread_ps[:, 0]).then_inc(att_kept, 1)

            dve.wait_ge(idx_loaded, 64)
            v.tensor_copy(src_rows, src_rows_i)
            v.tensor_copy(base_col, dst_rows_i[:, 0:1]).then_inc(rows_made, 1)
            v.tensor_scalar(mask_rows, mask_i, 0.0, None, ALU.is_lt).then_inc(rows_made, 1)
            dve.wait_ge(rows_made, 2)
            v.tensor_scalar(rel_rows, dst_rows_i, base_col, None, ALU.subtract)
            v.tensor_tensor(key_rows, number_i, src_rows, ALU.subtract).then_inc(rows_made, 1)
            dve.wait_ge(rows_turned, 1)
            for h in range(2):
                v.tensor_copy(gather_all[:, 0:NC, 4 * h:4 * h + 4].rearrange("p c j -> p j c"), turned[:, h]).then_inc(idx_kept, 1)
            dve.wait_ge(rows_made, 3)
            v.scalar_tensor_tensor(rel_rows, mask_rows, FAR, rel_rows, ALU.mult, ALU.add)
            v.tensor_tensor(key_rows, key_rows, mask_rows, ALU.mult).then_inc(rows_made, 1)
            dve.wait_ge(rows_made, 4)
            v.tensor_tensor(key_rows, key_rows, src_rows, ALU.add).then_inc(rows_made, 1)
            v.memset(dst_term[:, N:NPAD], 0.0)
            v.memset(key[:, NC:NC + 2], 0.0)
            v.memset(gather_all[:, NC:NC + SLOTS], 0)
            dve.wait_ge(rows_turned, 2)
            v.tensor_copy(base_i[:], base_ps)
            for a, kept in ((1, rel), (2, key)):
                for h in range(2):
                    last = v.tensor_copy(kept[:, 0:NC, 4 * h:4 * h + 4].rearrange("p c j -> p j c"), turned[:, 2 * a + h])
            last.then_inc(idx_made, 1)

            dve.wait_ge(idx_made, 1)
            def src_products(s, product, o, done):
                for j in range(TPC):
                    last = v.tensor_tensor_reduce(product[:, j], rows[:, s, j, :], w_att_a[:], 1.0, 0.0, ALU.mult, ALU.add,
                                                  o[:, j:j + 1])
                last.then_inc(done, 1)

            def src_terms(s, i, c):
                dve.wait_ge(gathered[s], i * (16 * TPC) + 16 * TPC)
                v.tensor_copy(gather_idx[:, s], chunk_of(gather_all, c + SLOTS)).then_inc(gather_idx_made, 1)
                src_products(s, (dups, same)[s % 2], src_term[:, s % 2], src_term_made)

            def weigh(q, c):
                dve.wait_ge(att_made, c + 1)
                for j in range(TPC):
                    last = v.scalar_tensor_tensor(hot[:, q, j, :], col[:], rel[:, bass.ds(c, 1), j:j + 1].rearrange("p c j -> p (c j)"),
                                                  att[:, q, j, :], ALU.is_equal, ALU.mult)
                last.then_inc(hot_made, 1)

            def add_sums(q, c, first):
                node = dve.value_load(base_i[0:1, bass.ds(c, 1)], min_val=0, max_val=N - 1)
                dve.wait_ge(summed, c + 1)
                if first:
                    dve.wait_ge(acc_x_zero, 1)
                    dve.wait_ge(accs_zero, 1)
                else:
                    dve.wait_ge(added, c)
                v.tensor_tensor(acc_x[:, bass.ds(node, P)], acc_x[:, bass.ds(node, P)], sum_ps[q], ALU.add)
                v.tensor_tensor(acc_w[:, bass.ds(node, P)], acc_w[:, bass.ds(node, P)], weight_ps[q], ALU.add).then_inc(added, 1)

            def first_loop(i, first, n_merged):
                for s in range(SLOTS):
                    src_terms(s, i, SLOTS * i + s)
                    if s == 0 and n_merged:
                        dve.wait_ge(merged, n_merged)
                    if first and s == 0:
                        v.memset(acc_x[:], 0.0).then_inc(acc_x_zero, 1)
                    if s >= 1:
                        weigh((s - 1) % 2, SLOTS * i + s - 1)
                    if s >= 2:
                        add_sums(s % 2, SLOTS * i + s - 2, first and s == 2)
                weigh(1, SLOTS * i + 3)
                add_sums(0, SLOTS * i + 2, False)
                add_sums(1, SLOTS * i + 3, False)

            dve.wait_ge(att_kept, 1)
            dve.wait_ge(idx_kept, 2)
            first_loop(0, True, 0)
            dve.wait_ge(w_loaded, 16 * N_W)
            v.tensor_tensor(b_gate[:], b_ih_sb[:, 0:2], b_hh_sb[:, 0:2], ALU.add)
            v.tensor_tensor(w_node_sb[:], w_node_sb[:], ident[:], ALU.add)
            v.tensor_scalar(diag[:, 1], ident[:], vecs[:, 3:4], None, ALU.mult).then_inc(weights_made, 1)
            v.tensor_scalar(left, rel[:], float(P), None, ALU.is_ge).then_inc(left_step, 1)
            dve.wait_ge(left_step, 1)
            v.scalar_tensor_tensor(left, rel[:], FAR / 2, left, ALU.is_lt, ALU.mult).then_inc(left_step, 1)
            dve.wait_ge(left_step, 2)
            v.scalar_tensor_tensor(left, rel[:], 0.0, left, ALU.is_lt, ALU.add).then_inc(left_step, 1)
            dve.wait_ge(left_step, 3)
            v.tensor_reduce(n_left[:], left, AX.XY, ALU.add).then_inc(left_step, 1)
            dve.wait_ge(left_counted, 1)
            v.tensor_copy(n_left_i[:], left_ps).then_inc(left_known, 1)
            with dve.Fori(1, MID) as i:
                first_loop(i, False, 0)

            def tiles(ap):
                return ap.unsqueeze(2).to_broadcast([P, TPC, P])

            def every(ap):
                return ap.unsqueeze(1).to_broadcast([P, TPC, P])

            dve.wait_ge(zeros_made, 2 * 16 * TABLES)

            dve.wait_ge(left_known, 1)
            with dve.If(dve.value_load(n_left_i[0:1, 0:1], min_val=0, max_val=E) > 0):
                dve.wait_ge(added, SLOTS * MID)
                v.tensor_copy(base_f, base_i[:]).then_inc(g_base, 1)
                dve.wait_ge(g_base_ps, 1)
                v.tensor_copy(base_bc, base_bc_ps).then_inc(g_base, 1)
                dve.wait_ge(g_base, 2)
                with dve.Fori(0, NC) as c:
                    v.tensor_copy(scatter_idx[:, 0], chunk_of(gather_all, c))
                    v.tensor_scalar(left_now, chunk_of(rel, c), base_bc[:, bass.ds(c, 1)], 1.0, ALU.add, ALU.add).then_inc(g_left, 1)
                    dve.wait_ge(g_left, 3 * c + 1)
                    v.tensor_tensor(left_now, left_now, chunk_of(left, c), ALU.mult).then_inc(g_left, 1)
                    dve.wait_ge(g_left, 3 * c + 2)
                    v.tensor_scalar(left_now, left_now, -1.0, None, ALU.add).then_inc(g_left, 1)
                    dve.wait_ge(g_left, 3 * c + 3)
                    v.tensor_copy(n_dups[:], left_now).then_inc(g_ready, 1)
                    dve.wait_ge(g_gathered, c * (16 * TPC) + 16 * TPC)
                    src_products(0, same, src_term[:, 0], g_src_term)
                    dve.wait_ge(g_src_term, c + 1)
                    dve.nop(nofuse=True)
                    with dve.Fori(0, NB) as b:
                        n = c * NB + b
                        v.tensor_tensor(hot[:, 0], every(col[:]), tiles(left_now), ALU.is_equal).then_inc(g_hot, 1)
                        dve.wait_ge(g_att, n + 1)
                        dve.wait_ge(g_hot, n + 1)
                        v.tensor_tensor(hot[:, 1], hot[:, 0], att[:, 0], ALU.mult)
                        v.tensor_scalar(left_now, left_now, -float(P), None, ALU.add).then_inc(g_weighted, 1)
                        dve.wait_ge(g_summed, n + 1)
                        for acc, bank in ((acc_x, sum_ps[0]), (acc_w, weight_ps[0]), (acc_in, sum_ps[1])):
                            last = v.tensor_tensor(acc[:, bass.ds(b * P, P)], acc[:, bass.ds(b * P, P)], bank, ALU.add)
                        last.then_inc(g_added, 1)
                        dve.wait_ge(g_added, n + 1)
            v.memset(n_dups[:], 0.0).then_inc(general_done, 1)
            dve.wait_ge(general_done, 1)

            def copy_keys(q, c):
                v.tensor_copy(key_now[:, q], chunk_of(key, c)).then_inc(keys_copied, 1)

            def find(q, s, c, first, second, first_quad):
                v.tensor_tensor(hot[:, q], every(col[:]), tiles(chunk_of(rel, c)), ALU.is_equal).then_inc(onehot_made, 1)
                if not first:
                    add_in(c - 1, second)
                dve.wait_ge(keys_spread, c + 1)
                if not first:
                    dve.wait_ge(merged, c)
                v.tensor_tensor(same[:], key_ps, tiles(chunk_of(key, c)), ALU.is_equal).then_inc(same_made, 1)
                dve.wait_ge(same_made, c + 1)
                v.tensor_tensor(dups[:], same[:], every(earlier[:]), ALU.mult).then_inc(dups_made, 1)
                copy_keys(q, c + 2)
                v.tensor_scalar(to_trash[:], chunk_of(key, c), -1.0, trash_row[:, 0:1], ALU.mult, ALU.add)
                dve.wait_ge(dups_made, c + 1)
                v.tensor_reduce(n_dups[:], dups[:], AX.X, ALU.add).then_inc(counted, 1)
                dve.wait_ge(counted, c + 1)
                v.scalar_tensor_tensor(moved[:], n_dups[:], 1.0, to_trash[:], ALU.min, ALU.mult).then_inc(moved_made, 1)
                dve.wait_ge(moved_made, c + 1)
                if not first_quad:
                    dve.wait_ge(scattered, c - 2)
                v.tensor_tensor(scatter_idx[:, s], moved[:], chunk_of(key, c), ALU.add).then_inc(scatter_idx_made, 1)

            def add_in(c, first):
                node = dve.value_load(base_i[0:1, bass.ds(c, 1)], min_val=0, max_val=N - 1)
                dve.wait_ge(in_summed, c + 1)
                if not first:
                    dve.wait_ge(in_added, c)
                v.tensor_tensor(acc_in[:, bass.ds(node, P)], acc_in[:, bass.ds(node, P)], in_ps, ALU.add
                                ).then_inc(in_added, 1)

            def pair(p, h, first, first_quad):
                find(0, 2 * h, 2 * p, first, False, first_quad)
                find(1, 2 * h + 1, 2 * p + 1, False, first, first_quad)

            copy_keys(0, 0)
            copy_keys(1, 1)
            for c in range(3):
                find(c % 2, (c + 2) % SLOTS, c, c == 0, c == 1, True)
                with dve.Fori(STOPS[c], STOPS[c + 1]) as i:
                    first_loop(i, False, c + 1)
            dve.wait_ge(added, NC)
            v.memset(n_dups[:], 0.0).then_inc(by_dst_done, 1)
            dve.wait_ge(by_dst_done, 1)

            def gru_pre(t):
                dve.wait_ge(reset_made, t + 1)
                v.scalar_tensor_tensor(tmp, new_h_bank, b_hh_sb[:, 2:3], reset, ALU.add, ALU.mult).then_inc(scaled, 1)
                dve.wait_ge(scaled, t + 1)
                v.tensor_tensor(pre, tmp, new_in_bank, ALU.add).then_inc(pre_made, 1)

            def gru_mix(t):
                nodes = bass.ds(t * GW, GW)
                dve.wait_ge(new_made, t + 1)
                v.tensor_tensor(tmp, xT_sb[:, nodes], new, ALU.subtract).then_inc(diff_made, 1)
                dve.wait_ge(diff_made, t + 1)
                dve.wait_ge(update_made, t + 1)
                v.tensor_tensor(tmp, tmp, update, ALU.mult).then_inc(mixed, 1)
                dve.wait_ge(mixed, t + 1)
                v.tensor_tensor(acc_x[:, nodes], tmp, new, ALU.add).then_inc(h_made, 1)
                dve.wait_ge(h_made, t + 1)
                v.bn_stats(stats[:, bass.ds(t * 6, 6)], acc_x[:, nodes]).then_inc(bn_stats_made, 1)

            def pair_with_gru(p, h):
                find(0, 2 * h, 2 * p, False, False, False)
                gru_pre(p - 2)
                find(1, 2 * h + 1, 2 * p + 1, False, False, False)
                gru_mix(p - 2)

            find(1, 1, 3, False, False, True)
            with dve.Fori(1, (GS + 1) // 2) as i:
                for h in range(2):
                    pair_with_gru(2 * i + h, 1 - h)
            gru_pre(GS - 1)
            gru_mix(GS - 1)

            dve.wait_ge(bn_stats_made, GS)
            v.bn_aggr(bn[:, 0:2], stats[:]).then_inc(bn_made[0], 1)
            dve.wait_ge(bn_made[1], 1)
            v.reciprocal(bn_inv, bn_std).then_inc(bn_made[2], 1)
            dve.wait_ge(bn_made[2], 1)
            v.tensor_tensor(bn_scale, bn_inv, vecs[:, 0:1], ALU.mult).then_inc(bn_made[3], 1)
            dve.wait_ge(bn_made[3], 1)
            v.tensor_tensor(bn_off, bn_mean, bn_scale, ALU.mult).then_inc(bn_made[4], 1)
            dve.wait_ge(bn_made[4], 1)
            v.tensor_tensor(bn_shift, vecs[:, 1:2], bn_off, ALU.subtract).then_inc(bn_made[5], 1)

            u, std, inv = agg, reset, tmp

            def pair_with_ln(t, h, first):
                nodes = bass.ds(t * GW, GW)
                dve.wait_ge(u_made, t + 1)
                if not first:
                    dve.wait_ge(centered, t)
                v.tensor_tensor(y, u, xT_sb[:, nodes], ALU.add).then_inc(y_made, 1)
                pair(t + (GS + 1), h, False, False)
                dve.wait_ge(std_made, t + 1)
                v.reciprocal(inv, std).then_inc(inv_made, 1)
                dve.wait_ge(inv_made, t + 1)
                v.tensor_tensor(acc_x[:, nodes], center_bank, inv, ALU.mult).then_inc(x1_made, 1)

            pair_with_ln(0, 1, True)
            with dve.Fori(0, GS // 2) as i:
                for h in range(2):
                    pair_with_ln(2 * i + (h + 1), h, False)
            pair(PAIRS - 1, 0, False, False)
            add_in(NC - 1, False)

            dve.wait_ge(bias_spread, 1)
            v.tensor_copy(bias_all[:], spread_ps[:, 1]).then_inc(bias_kept, 1)
            dve.wait_ge(bias_kept, 1)

            def add_z(h, g, blocks):
                dve.wait_ge(z_turned, g + 1)
                v.tensor_tensor(by_node[:, bass.ds(g * GROUP, blocks)], turned_z[h][:, 0:blocks],
                                bias_all[:].unsqueeze(1).to_broadcast([P, blocks, P]), ALU.add).then_inc(z_added, 1)

            with dve.Fori(0, NG // 2) as i:
                for h in range(2):
                    add_z(h, 2 * i + h, GROUP)
            add_z(0, NG, 1)

            def moments(h, g, blocks, first):
                dve.wait_ge(out_ps, g + 1)
                dve.wait_ge(z_added, NG + 1)
                if not first:
                    dve.wait_ge(o_made, g - 1)
                v.tensor_tensor(biased[:, h, 0:blocks], out_bank[h][:, 0:blocks], by_node[:, bass.ds(g * GROUP, blocks)], ALU.add
                                ).then_inc(o_added, 1)
                dve.wait_ge(o_added, g + 1)
                for b in range(blocks):
                    last = v.bn_stats(o_stat[:, h, b], biased[:, h, b])
                last.then_inc(o_stats_made, 1)
                dve.wait_ge(o_stats_made, g + 1)
                dve.nop(nofuse=True)
                for b in range(blocks):
                    last = v.bn_aggr(o_mv[:, h, b], o_stat[:, h, b])
                last.then_inc(o_mv_made, 1)

            def scale_shift(h, g, blocks):
                dve.wait_ge(o_std_made, g + 1)
                v.reciprocal(o_inv[:, h, 0:blocks], o_std[:, h, 0:blocks]).then_inc(o_inv_made, 1)
                dve.wait_ge(o_inv_made, g + 1)
                v.scalar_tensor_tensor(o_shift[:, h, 0:blocks], o_mv[:, h, 0:blocks, 0], -1.0, o_inv[:, h, 0:blocks],
                                       ALU.mult, ALU.mult).then_inc(o_shift_made, 1)

            def four_groups(i, first):
                for s in range(SLOTS):
                    moments(s % 2, SLOTS * i + s, GROUP, first and s < 2)
                    scale_shift(s % 2, SLOTS * i + s, GROUP)

            four_groups(0, True)
            with dve.Fori(1, NG // SLOTS) as i:
                four_groups(i, False)
            moments(0, NG, 1, False)
            scale_shift(0, NG, 1)

        @block.tensor
        def _(pe):
            mm = nc.tensor.matmul

            def turn(a, by_chunk):
                tile = by_chunk.rearrange("c (p j) -> c j p", j=TPC)
                for j in range(TPC):
                    last = nc.tensor.transpose(turned[:, 2 * a + j // 4, j % 4], tile[:, j], ident[0:NC, 0:NC])
                return last

            pe.wait_ge(consts_made, 3)
            pe.wait_ge(att_diag_made, 1)
            mm(spread_ps[:, 0], ones[:], diag[:, 0], start=True, stop=True).then_inc(att_spread, 1)

            pe.wait_ge(rows_made, 1)
            turn(0, src_rows).then_inc(rows_turned, 1)
            pe.wait_ge(rows_made, 5)
            nc.tensor.transpose(base_ps, base_col, ident[0:NC, 0:NC])
            turn(1, rel_rows)
            turn(2, key_rows).then_inc(rows_turned, 1)

            pe.wait_ge(x_loaded, 16)
            pe.wait_ge(idx_kept, 2)

            def dst_terms(q, t, width):
                mm(ps[:, q, 0:width], w_att_sb[:, 1:2].to_broadcast([P, P]), xT_sb[:, bass.ds(t * AW, width)],
                   start=True, stop=True).then_inc(dst_term_ps, 1)

            dst_terms(0, 0, AW)
            dst_terms(1, 1, AW)
            with pe.Fori(1, AS // 2) as i:
                for q in range(2):
                    pe.wait_ge(dst_term_sb, 2 * i + (q - 1))
                    dst_terms(q, 2 * i + q, AW)
            pe.wait_ge(dst_term_sb, AS - 1)
            dst_terms(0, AS, GW)
            pe.wait_ge(dst_term_sb, AS + 1)

            def window_sum(bank, values, weights):
                for j in range(TPC):
                    last = mm(bank, values(j), weights[:, j, :], start=(j == 0), stop=(j == TPC - 1))
                return last

            pe.wait_ge(idx_made, 1)
            def sums(i):
                for s in range(SLOTS):
                    q = s % 2
                    pe.wait_ge(hot_made, SLOTS * i + s + 1)
                    window_sum(sum_ps[q], lambda j: rows[:, s, j, :], hot[:, q]).then_inc(rows_used, 1)
                    window_sum(weight_ps[q], lambda j: ones[:, 0:1], hot[:, q]).then_inc(summed, 1)

            sums(0)
            pe.wait_ge(left_step, 4)
            mm(left_ps, n_left[:], ones[:, 0:1], start=True, stop=True).then_inc(left_counted, 1)
            with pe.Fori(1, MID) as i:
                sums(i)

            pe.wait_ge(left_known, 1)
            with pe.If(pe.value_load(n_left_i[0:1, 0:1], min_val=0, max_val=E) > 0):
                pe.wait_ge(g_base, 1)
                mm(base_bc_ps, ones[0:1, :], base_f, start=True, stop=True).then_inc(g_base_ps, 1)
                with pe.Fori(0, NC) as c:
                    pe.wait_ge(g_loaded, 16 * c + 16)
                    pe.nop(nofuse=True)
                    with pe.Fori(0, NB) as b:
                        pe.wait_ge(g_weighted, c * NB + b + 1)
                        window_sum(sum_ps[0], lambda j: rows[:, 0, j, :], hot[:, 1])
                        window_sum(weight_ps[0], lambda j: ones[:, 0:1], hot[:, 1])
                        window_sum(sum_ps[1], lambda j: ea[:, 0, j, :], hot[:, 0]).then_inc(g_summed, 1)

            def spread_keys(q, c):
                pe.wait_ge(keys_copied, c + 1)
                for j in range(TPC):
                    last = nc.tensor.transpose(key_ps[:, j], key_now[:, q, j:j + 1].to_broadcast([P, P]), ident[:])
                last.then_inc(keys_spread, 1)

            def chunk(q, i, first):
                c = 2 * i + q
                pe.wait_ge(ea_loaded[q], 16 * i + 16)
                pe.wait_ge(onehot_made, c + 1)
                if not first:
                    pe.wait_ge(in_added, c)
                window_sum(in_ps, lambda j: ea[:, q, j, :], hot[:, q]).then_inc(in_summed, 1)
                pe.wait_ge(same_made, c + 1)
                spread_keys(1 - q, c + 1)
                if not first:
                    pe.wait_ge(merged_kept, c)
                for j in range(TPC):
                    last = mm(merge_ps[:, j], same[:, j, :], ea[:, q, j, :], start=True, stop=True)
                last.then_inc(merged, 1)

            spread_keys(0, 0)
            for c in range(3):
                chunk(c % 2, c // 2, c == 0)
                with pe.Fori(STOPS[c], STOPS[c + 1]) as i:
                    sums(i)

            def gru_agg(t, first):
                nodes = bass.ds(t * GW, GW)
                if not first:
                    pe.wait_ge(reset_made, t)
                mm(agg_bank, w_msg_sb[:], acc_x[:, nodes], start=True, stop=False)
                mm(agg_bank, b_msg_row[:], acc_w[:, nodes], start=False, stop=True).then_inc(agg_ps, 1)

            def gru_gates(t, first):
                nodes = bass.ds(t * GW, GW)
                pe.wait_ge(agg_sb, t + 1)
                if not first:
                    pe.wait_ge(pre_made, t)
                    pe.wait_ge(update_made, t)
                for g, bank in enumerate((reset_bank, update_bank)):
                    mm(bank, w_ih_sb[:, g * P:(g + 1) * P], agg, start=True, stop=False)
                    mm(bank, w_hh_sb[:, g * P:(g + 1) * P], xT_sb[:, nodes], start=False, stop=True)
                mm(new_in_bank, w_ih_sb[:, 2 * P:], agg, start=True, stop=True)
                mm(new_h_bank, w_hh_sb[:, 2 * P:], xT_sb[:, nodes], start=True, stop=True).then_inc(gates_ps, 1)

            def pair_with_gru(i):
                chunk(0, i, False)
                gru_agg(i - 1, False)
                chunk(1, i, False)
                gru_gates(i - 1, False)

            pe.wait_ge(weights_made, 1)
            chunk(1, 1, False)
            pe.wait_ge(by_dst_done, 1)
            gru_agg(0, True)
            gru_gates(0, True)
            with pe.Fori(2, GS + 1) as i:
                pair_with_gru(i)

            def pair_with_ln(t, first):
                chunk(0, t + (GS + 1), False)
                pe.wait_ge(y_made, t + 1)
                if not first:
                    pe.wait_ge(x1_made, t)
                mm(center_bank, center[:], y, start=True, stop=True).then_inc(centered, 1)
                chunk(1, t + (GS + 1), False)
                pe.wait_ge(squared, t + 1)
                mm(var_bank, mean_w[:], sq, start=True, stop=True).then_inc(var_ps, 1)

            pe.wait_ge(pre_made, GS)
            pe.wait_ge(update_made, GS)
            pair_with_ln(0, True)
            with pe.Fori(1, GS) as t:
                pair_with_ln(t, False)
            chunk(0, PAIRS - 1, False)
            chunk(1, PAIRS - 1, False)

            def project(h, g, blocks, first):
                nodes = bass.ds(g * (GROUP * P), blocks * P)
                if not first:
                    pe.wait_ge(z_kept, g - 1)
                mm(ps[:, h, 0:blocks * P], w_node_sb[:], acc_x[:, nodes], start=True, stop=False)
                mm(ps[:, h, 0:blocks * P], w_in_sb[:], acc_in[:, nodes], start=False, stop=True).then_inc(z_ps, 1)

            def turn_z(h, g, blocks, first):
                pe.wait_ge(z_kept, g + 1)
                if not first:
                    pe.wait_ge(z_added, g - 1)
                for b in range(blocks):
                    last = nc.tensor.transpose(turned_z[h][:, b], z_sb[:, h, b], ident[:])
                last.then_inc(z_turned, 1)

            pe.wait_ge(x1_made, GS)
            mm(spread_ps[:, 1], ones[:], diag[:, 1], start=True, stop=False)
            mm(spread_ps[:, 1], vecs[:, 2:3].to_broadcast([P, P]), w_glob_sb[:], start=False, stop=True).then_inc(bias_spread, 1)
            pe.wait_ge(in_added, NC)
            pe.wait_ge(same_made, NC)
            for i, loop in ((0, None), (1, NG // 2)):
                if loop is None:
                    project(0, 0, GROUP, True)
                    project(1, 1, GROUP, True)
                    turn_z(0, 0, GROUP, True)
                    turn_z(1, 1, GROUP, True)
                else:
                    with pe.Fori(1, loop) as i:
                        for step in (project, turn_z):
                            for h in range(2):
                                step(h, 2 * i + h, GROUP, False)
            project(0, NG, 1, False)
            turn_z(0, NG, 1, False)

            def sum_tables(s, g, blocks, first):
                pe.wait_ge(tabs_halved, g + 1)
                if not first:
                    pe.wait_ge(tabs_kept, g - 1)
                for b in range(blocks):
                    for k in range(2):
                        last = mm(summed_T[s % 2][:, b], tabs[s][:, k, b], ident[:], start=(k == 0), stop=(k == 1))
                last.then_inc(tabs_summed, 1)

            def project_sums(h, g, blocks, first):
                pe.wait_ge(tabs_kept, g + 1)
                if not first:
                    pe.wait_ge(o_added, g - 1)
                else:
                    pe.wait_ge(bias_kept, 1)
                for b in range(blocks):
                    last = mm(out_bank[h][:, b], sums_T[:, h, b], w_out_sb[:], start=True, stop=True)
                last.then_inc(out_ps, 1)

            def four_groups(i, first):
                sum_tables(0, SLOTS * i, GROUP, first)
                for s in range(SLOTS):
                    if s < SLOTS - 1:
                        sum_tables(s + 1, SLOTS * i + (s + 1), GROUP, first and s == 0)
                    project_sums(s % 2, SLOTS * i + s, GROUP, first and s < 2)

            four_groups(0, True)
            with pe.Fori(1, NG // SLOTS) as i:
                four_groups(i, False)
            sum_tables(0, NG, 1, False)
            project_sums(0, NG, 1, False)


def kernel(**inputs):
    import numpy as np
    import concourse.bacc as bacc
    from concourse.bass_utils import run_bass_kernel_spmd

    a = {k: np.asarray(v) for k, v in inputs.items()}
    order = {
        "x": a["x"], "xT": a["x"].T, "src": a["src"], "dst": a["dst"], "edge_attr": a["edge_attr_128"],
        "W_msg": a["L0_gnn_W_msg"], "b_msg": a["L0_gnn_b_msg"], "W_att": a["L0_gnn_W_att"], "b_att": a["L0_gnn_b_att"],
        "W_ihT": a["L0_gnn_W_ih"].T, "b_ih": a["L0_gnn_b_ih"], "W_hhT": a["L0_gnn_W_hh"].T, "b_hh": a["L0_gnn_b_hh"],
        "gamma": a["L0_gnn_gamma"], "beta": a["L0_gnn_beta"], "glob": a["L1_gnn_global_features"],
        "W_nodeT": a["L1_gnn_W_node"].T, "W_inT": a["L1_gnn_W_incoming"].T, "W_outT": a["L1_gnn_W_outgoing"].T,
        "W_globT": a["L1_gnn_W_global"].T, "bias": a["L1_gnn_bias"],
    }
    nc = bacc.Bacc("TRN2", target_bir_lowering=False, num_devices=1)
    arrays, args = {}, []
    for name, v in order.items():
        v = np.ascontiguousarray(v)
        arrays[f"in_{name}"] = v
        args.append(nc.dram_tensor(f"in_{name}", v.shape, mybir.dt.from_np(v.dtype), kind="ExternalInput").ap())
    args.append(nc.dram_tensor("out_x", a["x"].shape, F32, kind="ExternalOutput").ap())
    gnn_two_layers(nc, *args)
    r = run_bass_kernel_spmd(nc, [arrays], core_ids=[0])
    return r.results[0]["out_x"]
```

```python
from contextlib import ExitStack

import concourse.bass as bass
from concourse import mybir

ALU = mybir.AluOpType
ACT = mybir.ActivationFunctionType
AX = mybir.AxisListType
F32 = mybir.dt.float32
I32 = mybir.dt.int32
U32 = mybir.dt.uint32

P = 128
TPC = 8
CHUNK = P * TPC
SLOTS = 4
GROUP = 4
TABLES = 4
BANK = 512
GW = 250
AW = 500
EPS = 1e-5
FAR = 20000.0


def gnn_two_layers(nc, x, xT, src, dst, edge_attr, W_msg, b_msg, W_att, b_att, W_ihT, b_ih, W_hhT, b_hh,
                   gamma, beta, glob, W_nodeT, W_inT, W_outT, W_globT, bias, out):
    N = x.shape[0]
    E = edge_attr.shape[0]
    NC = -(-E // CHUNK)
    WHOLE = NC - 1
    LAST = E - CHUNK
    DONE = WHOLE * CHUNK - LAST
    NB = -(-N // P)
    NPAD = (NB + 1) * P
    TRASH = NB * P
    MASKED = TRASH + P
    ROWS = MASKED + 2 * P
    GS = N // GW
    PAIRS = NC // 2
    AS = N // AW
    X_SPLIT = AS // 2
    ITERS = NC // SLOTS
    MID = ITERS // 2
    STOPS = (MID, MID + ITERS // 6, MID + 2 * (ITERS // 6), ITERS)
    assert NC % SLOTS == 0 and N % GW == 0 and GS % 2 == 1 and NC <= P and DONE <= 2 * P
    NG = NB // GROUP
    assert N - AS * AW == GW and AS % 4 == 0 and X_SPLIT % 2 == 0 and ROWS % P == 0 and NB % GROUP == 1 and NG == 6 + 2 * (NPAD // (TABLES * GROUP * P))
    assert NC % 4 == 0 and 2 * GS + 2 == PAIRS and TABLES == 4

    with ExitStack() as ctx:
        def sb(name, shape, dt=F32):
            return ctx.enter_context(nc.sbuf_tensor(name, shape, dt))

        def sem(name):
            return ctx.enter_context(nc.semaphore(name))

        ps = ctx.enter_context(nc.psum_tensor("ps", [P, 8, BANK], F32))

        tables = [nc.dram_tensor(f"by_src_{k}", [ROWS, P], F32, kind="Internal").ap() for k in range(TABLES)]

        iota_i = sb("iota_i", [P, P], I32)
        part_i = sb("part_i", [P, 1], I32)
        col = sb("col", [P, P])
        part = sb("part", [P, 1])
        trash_row = sb("trash_row", [P, 1])
        ident = sb("ident", [P, P])
        earlier = sb("earlier", [P, P])
        ones = sb("ones", [P, P])
        mean_w = sb("mean_w", [P, P])
        center = sb("center", [P, P])
        eps = sb("eps", [P, 1])

        base_i = sb("base_i", [1, NC], I32)
        gather_all = sb("gather_all", [P, NC + SLOTS, TPC], U32)
        rel = sb("rel", [P, NC, TPC])
        key = sb("key", [P, NC + 2, TPC])
        key_now = sb("key_now", [P, 2, TPC])
        n_left = sb("n_left", [P, 1])
        n_left_i = sb("n_left_i", [1, 1], I32)
        gather_idx = sb("gather_idx", [P, SLOTS, TPC], U32)
        scatter_idx = sb("scatter_idx", [P, SLOTS, TPC], U32)

        xT_sb = sb("xT_sb", [P, NB * P])
        by_node = xT_sb[:].rearrange("p (b f) -> p b f", f=P)
        w_att_sb = sb("w_att_sb", [P, 2])
        diag = sb("diag", [P, P])
        w_att_a = sb("w_att_a", [P, P])
        b_att_sb = sb("b_att_sb", [P, 1])
        w_msg_sb = sb("w_msg_sb", [P, P])
        b_msg_row = sb("b_msg_row", [1, P])
        w_ih_sb = sb("w_ih_sb", [P, 3 * P])
        w_hh_sb = sb("w_hh_sb", [P, 3 * P])
        b_ih_sb = sb("b_ih_sb", [P, 3])
        b_hh_sb = sb("b_hh_sb", [P, 3])
        b_gate = sb("b_gate", [P, 2])
        vecs = sb("vecs", [P, 4])
        w_glob_sb = sb("w_glob_sb", [P, P])
        w_node_sb = sb("w_node_sb", [P, P])
        w_in_sb = sb("w_in_sb", [P, P])
        w_out_sb = sb("w_out_sb", [P, P])
        bias_col = sb("bias_col", [P, 1])

        dst_term = sb("dst_term", [P, NPAD])
        acc_x = sb("acc_x", [P, NPAD])
        acc_w = sb("acc_w", [1, NPAD])
        acc_in = sb("acc_in", [P, NPAD])

        rows = sb("rows", [P, SLOTS, TPC, P])
        ea = sb("ea", [P, 2, TPC, P])
        src_term = sb("src_term", [P, 2, TPC])
        att = sb("att", [P, SLOTS, TPC, P])
        hot = sb("hot", [P, 2, TPC, P])
        same = sb("same", [P, TPC, P])
        dups = sb("dups", [P, TPC, P])
        n_dups = sb("n_dups", [P, TPC])
        moved = sb("moved", [P, TPC])
        to_trash = sb("to_trash", [P, TPC])
        stats = sb("stats", [P, GS * 6])
        bn = sb("bn", [P, 7])
        bn_mean, bn_var, bn_std, bn_inv, bn_scale, bn_off, bn_shift = (bn[:, k:k + 1] for k in range(7))

        src_rows, rel_rows, key_rows, mask_rows = (acc_x[0:NC, k * CHUNK:(k + 1) * CHUNK] for k in range(4))
        hot_c = hot[0:NC].rearrange("c s j f -> c s (j f)")
        src_rows_i, dst_rows_i = (hot_c[:, s].bitcast(I32) for s in range(2))
        att_c = att[0:NC].rearrange("c s j f -> c s (j f)")
        mask_i, number_i = (att_c[:, s].bitcast(I32) for s in range(2))
        base_col = n_dups[0:NC, 0:1]

        agg, reset, update, new, pre, tmp, sq, y = (dst_term[:, k * GW:(k + 1) * GW] for k in range(8))
        D = 8 * GW
        z_sb, more, yet_more, sums_T = (
            dst_term[:, D + k * 2 * BANK:D + (k + 1) * 2 * BANK].rearrange("p (h b f) -> p h b f", h=2, f=P) for k in range(4))
        out_rows = [buf[:, h] for buf in (z_sb, more, yet_more) for h in range(2)]
        spare = dst_term[:, D + 8 * BANK:D + 8 * BANK + SLOTS * GROUP * 11]
        o_stat = spare[:, 0:SLOTS * GROUP * 6].rearrange("p (s b k) -> p s b k", s=SLOTS, k=6)
        o_mv = spare[:, SLOTS * GROUP * 6:SLOTS * GROUP * 8].rearrange("p (s b k) -> p s b k", s=SLOTS, k=2)
        o_std, o_inv, o_shift = (
            spare[:, SLOTS * GROUP * k:SLOTS * GROUP * (k + 1)].rearrange("p (s b) -> p s b", s=SLOTS) for k in (8, 9, 10))
        places = [buf[:, 2 * h:2 * h + 2].rearrange("p s j f -> p (s j) f") for buf, n in ((rows, 2), (att, 2), (ea, 1), (hot, 1))
                  for h in range(n)]
        places += [buf[:, k * TABLES * GROUP * P:(k + 1) * TABLES * GROUP * P].rearrange("p (r f) -> p r f", f=P)
                   for buf in (acc_x, acc_in) for k in range(NPAD // (TABLES * GROUP * P))]
        tabs = [place.rearrange("p (k b) f -> p k b f", k=TABLES) for place in places + places[0:1]]
        whole = [buf[:, GROUP * h:GROUP * (h + 1)] for buf in (same, dups) for h in range(2)]
        base_bc = dups[:, 0, 0:NC]
        base_f = dups[0:1, 1, 0:NC]
        left_now = moved[:]
        left = ea[:, 1].rearrange("p j f -> p (j f)")[:, 0:NC * TPC].rearrange("p (c j) -> p c j", j=TPC)

        att_loaded = sem("att_loaded")
        iotas_made, consts_made = sem("iotas_made"), sem("consts_made")
        idx_loaded, w_loaded, x_loaded = sem("idx_loaded"), sem("w_loaded"), [sem(f"x_loaded{h}") for h in range(2)]
        first_idx_loaded = sem("first_idx_loaded")
        idx_kept, acc_x_zero = sem("idx_kept"), sem("acc_x_zero")
        rows_made, rows_turned, idx_made = sem("rows_made"), sem("rows_turned"), sem("idx_made")
        att_diag_made, att_spread, att_kept, weights_made = (
            sem(n) for n in ("att_diag_made", "att_spread", "att_kept", "weights_made"))
        dst_term_ps, dst_term_sb, accs_zero = sem("dst_term_ps"), sem("dst_term_sb"), sem("accs_zero")
        left_step, left_counted, left_known = sem("left_step"), sem("left_counted"), sem("left_known")
        gather_idx_made = sem("gather_idx_made")
        gathered = [sem(f"gathered{s}") for s in range(SLOTS)]
        src_term_made, att_made, hot_made = sem("src_term_made"), sem("att_made"), sem("hot_made")
        summed, added = sem("summed"), sem("added")
        g_base, g_base_ps, g_left, g_ready, g_loaded, g_gathered = (
            sem(n) for n in ("g_base", "g_base_ps", "g_left", "g_ready", "g_loaded", "g_gathered"))
        g_src_term, g_hot, g_att, g_weighted, g_summed, g_added = (
            sem(n) for n in ("g_src_term", "g_hot", "g_att", "g_weighted", "g_summed", "g_added"))
        general_done, by_dst_done, rows_used = sem("general_done"), sem("by_dst_done"), sem("rows_used")
        zeros_made = sem("zeros_made")
        table_free = [sem(f"table_free{k}") for k in range(TABLES)]
        ea_loaded = [sem(f"ea_loaded{q}") for q in range(2)]
        keys_copied, keys_spread, onehot_made, same_made, dups_made = (
            sem(n) for n in ("keys_copied", "keys_spread", "onehot_made", "same_made", "dups_made"))
        counted, moved_made, scatter_idx_made = sem("counted"), sem("moved_made"), sem("scatter_idx_made")
        in_summed, in_added, merged, merged_kept = (
            sem("in_summed"), sem("in_added"), sem("merged"), sem("merged_kept"))
        scattered = sem("scattered")
        agg_ps, agg_sb, gates_ps, reset_made, update_made, scaled, pre_made, new_made, diff_made, mixed, h_made, bn_stats_made = (
            sem(n) for n in ("agg_ps", "agg_sb", "gates_ps", "reset_made", "update_made", "scaled", "pre_made", "new_made",
                             "diff_made", "mixed", "h_made", "bn_stats_made"))
        bn_made = [sem(f"bn_made{k}") for k in range(7)]
        u_made, y_made, centered, squared, var_ps, std_made, inv_made, x1_made = (
            sem(n) for n in ("u_made", "y_made", "centered", "squared", "var_ps", "std_made", "inv_made", "x1_made"))
        tabs_loaded = [sem(f"tabs_loaded{s}") for s in range(SLOTS)]
        x1_part_ps, x1_part_kept = sem("x1_part_ps"), sem("x1_part_kept")
        in_part_ps, z_made, z_turned, z_kept = (sem(n) for n in ("in_part_ps", "z_made", "z_turned", "z_kept"))
        tabs_halved, even_summed, odd_summed, sums_turned, sums_kept, out_ps = (
            sem(n) for n in ("tabs_halved", "even_summed", "odd_summed", "sums_turned", "sums_kept", "out_ps"))
        o_added, o_stats_made, o_mv_made, o_std_made, o_inv_made, o_shift_made, o_made = (
            sem(n) for n in ("o_added", "o_stats_made", "o_mv_made", "o_std_made", "o_inv_made", "o_shift_made", "o_made"))
        stored = [sem(f"stored{r}") for r in range(len(out_rows))]

        turned = ps[:, 0:6, 0:4 * NC].rearrange("p b (j c) -> p b j c", c=NC)
        base_ps = ps[0:1, 6, 0:NC]
        spread_ps = ps[:, 7, 0:P]
        sum_ps = [ps[:, 5 + q, 0:P] for q in range(2)]
        weight_ps = [ps[0:1, 5 + q, P:2 * P] for q in range(2)]
        left_ps, bias_ps, base_bc_ps = ps[0:1, 7, 0:1], ps[:, 7, 1:2], ps[:, 7, 0:NC]
        key_ps = ps[:, 0:2].rearrange("p b (j f) -> p (b j) f", f=P)
        in_ps = ps[:, 2, 0:P]
        merge_ps = ps[:, 3:5].rearrange("p b (j f) -> p (b j) f", f=P)
        agg_bank, reset_bank, update_bank = ps[:, 5, 0:GW], ps[:, 5, GW:2 * GW], ps[:, 6, 0:GW]
        new_in_bank, new_h_bank = ps[:, 7, 0:GW], ps[:, 7, GW:2 * GW]
        center_bank, var_bank, x1_part_bank = ps[:, 5, 0:GW], ps[:, 6, 0:GW], ps[:, 7, 0:GW]

        turned_z = [ps[:, bank].rearrange("p (b f) -> p b f", f=P) for bank in (2, 7)]
        summed_T = [ps[:, 4 + h].rearrange("p (b f) -> p b f", f=P) for h in range(2)]
        out_bank = [ps[:, 6 + h].rearrange("p (b f) -> p b f", f=P) for h in range(2)]

        def chunk_of(array, c):
            return array[:, bass.ds(c, 1)].rearrange("p c j -> p (c j)")

        def group_blocks(g):
            return GROUP if g < NG else 1

        def column(a):
            return a.rearrange("(p o) -> p o", o=1)

        small_loads = [(w_msg_sb[:], W_msg), (b_msg_row[:], b_msg.rearrange("(o d) -> o d", o=1)),
                       (w_ih_sb[:], W_ihT), (w_hh_sb[:], W_hhT),
                       (vecs[:, 0:1], column(gamma)), (vecs[:, 1:2], column(beta)),
                       (vecs[:, 2:3], column(glob[0])), (vecs[:, 3:4], column(bias)),
                       (w_glob_sb[:], W_globT), (w_node_sb[:], W_nodeT), (w_in_sb[:], W_inT), (w_out_sb[:], W_outT),
                       *[(b_ih_sb[:, g:g + 1], column(b_ih[g * P:(g + 1) * P])) for g in range(3)],
                       *[(b_hh_sb[:, g:g + 1], column(b_hh[g * P:(g + 1) * P])) for g in range(3)]]

        block = ctx.enter_context(nc.Block())

        @block.sync
        def _(sp):
            sp.dma_start(gather_idx[:].bitcast(I32), src[0:SLOTS * CHUNK].rearrange("(c p j) -> p c j", p=P, j=TPC)
                         ).then_inc(first_idx_loaded, 16)
            sp.dma_start(src_rows_i[0:WHOLE], src[0:WHOLE * CHUNK].rearrange("(c e) -> c e", e=CHUNK)).then_inc(idx_loaded, 16)
            sp.dma_start(dst_rows_i[0:WHOLE], dst[0:WHOLE * CHUNK].rearrange("(c e) -> c e", e=CHUNK)).then_inc(idx_loaded, 16)
            sp.dma_start(src_rows_i[WHOLE:NC], src[LAST:E].rearrange("(c e) -> c e", c=1)).then_inc(idx_loaded, 16)
            sp.dma_start(dst_rows_i[WHOLE:NC], dst[LAST:E].rearrange("(c e) -> c e", c=1)).then_inc(idx_loaded, 16)
            for h, (first, end) in enumerate(((0, X_SPLIT * AW), (X_SPLIT * AW, N))):
                sp.dma_start(xT_sb[:, first:end], xT[:, first:end]).then_inc(x_loaded[h], 16)

            for o, a in small_loads:
                sp.dma_start(o, a).then_inc(w_loaded, 16)

            def edges_from(first_edge):
                return edge_attr[bass.ds(first_edge, CHUNK)].rearrange("(p j) f -> p j f", j=TPC)

            sp.wait_ge(accs_zero, 2)
            for k in range(TABLES):
                sp.wait_ge(hot_made, (k + 1) * (SLOTS * MID // (TABLES + 1)))
                flat = tables[k].rearrange("(p a) f -> p (a f)", p=P)
                sp.dma_start(flat[:, 0:NPAD], acc_in[:]).then_inc(zeros_made, 16)
                sp.dma_start(flat[:, NPAD:ROWS], acc_in[:, 0:ROWS - NPAD]).then_inc(zeros_made, 16)

            sp.wait_ge(left_known, 1)
            with sp.If(sp.value_load(n_left_i[0:1, 0:1], min_val=0, max_val=E) > 0):
                with sp.Fori(0, WHOLE) as c:
                    sp.wait_ge(g_ready, c + 1)
                    sp.dma_start(ea[:, 0], edges_from(c * CHUNK)).then_inc(g_loaded, 16)
                sp.wait_ge(g_ready, NC)
                sp.dma_start(ea[:, 0], edges_from(LAST)).then_inc(g_loaded, 16)
                sp.wait_ge(g_added, NC * NB)

            def load(q, c, first_edge):
                sp.dma_start(ea[:, q], edges_from(first_edge)).then_inc(ea_loaded[q], 16)

            load(0, 0, 0)
            sp.wait_ge(general_done, 1)
            load(1, 1, CHUNK)
            with sp.Fori(1, PAIRS - 1) as i:
                for q in range(2):
                    sp.wait_ge(merged, 2 * i + (q - 1))
                    load(q, 2 * i + q, i * (2 * CHUNK) + q * CHUNK)
            sp.wait_ge(merged, NC - 3)
            load(0, NC - 2, (NC - 2) * CHUNK)
            sp.wait_ge(merged, NC - 2)
            load(1, NC - 1, LAST)

            sp.wait_ge(merged, NC)

            def store(g):
                sp.wait_ge(o_made, g + 1)
                r, first, end = g % len(out_rows), g * GROUP * P, min(N, (g + 1) * GROUP * P)
                blocks = group_blocks(g)
                sp.dma_start(out[first:end].rearrange("(b p) f -> p b f", b=blocks),
                             out_rows[r][0:(end - first) // blocks, 0:blocks]).then_inc(stored[r], 16)

            for g in range(NG + 1):
                s, blocks = g % SLOTS, group_blocks(g)
                if g >= SLOTS:
                    sp.wait_ge(tabs_loaded[s], 16 * TABLES * (g // SLOTS))
                if g == len(places) - 2 * (NPAD // (TABLES * GROUP * P)):
                    sp.wait_ge(z_made, NG + 1)
                if g == NG:
                    sp.wait_ge(even_summed, 1)
                for k in range(TABLES):
                    if g == 0:
                        sp.wait_ge(table_free[k], 16 * (NC * TPC // TABLES))
                    sp.dma_start(tabs[g][:, k, 0:blocks],
                                 tables[k][g * GROUP * P:(g * GROUP + blocks) * P].rearrange("(b p) f -> p b f", p=P)
                                 ).then_inc(tabs_loaded[s], 16)
                if g >= 2 * SLOTS:
                    store(g - 2 * SLOTS)
            for g in range(NG + 1 - 2 * SLOTS, NG + 1):
                store(g)
            for r in range(len(out_rows)):
                sp.wait_ge(stored[r], 16 * ((NG - r) // len(out_rows) + 1))

        @block.gpsimd
        def _(pool):
            nc.gpsimd.iota(iota_i[:], [[1, P]], base=0, channel_multiplier=0)
            nc.gpsimd.iota(part_i[:], [[1, 1]], base=0, channel_multiplier=1)
            nc.gpsimd.iota(mask_i, [[1, CHUNK]], base=WHOLE * CHUNK - DONE, channel_multiplier=-CHUNK)
            nc.gpsimd.iota(number_i, [[1, CHUNK]], base=MASKED, channel_multiplier=0).then_inc(iotas_made, 1)

            def gather(idx, s, done):
                for j in range(TPC):
                    pool.indirect_dma_start(rows[:, s, j, :], None, x,
                                            bass.IndirectOffsetOnAxis(ap=idx[:, s, j:j + 1], axis=0)
                                            ).then_inc(done, 16)

            pool.wait_ge(first_idx_loaded, 16)
            for s in range(SLOTS):
                gather(gather_idx, s, gathered[s])

            def gather_four(i):
                for s in range(SLOTS):
                    pool.wait_ge(rows_used, SLOTS * i + (s + 1 - SLOTS))
                    pool.nop(nofuse=True)
                    pool.wait_ge(gather_idx_made, SLOTS * i + (s + 1 - SLOTS))
                    pool.nop(nofuse=True)
                    gather(gather_idx, s, gathered[s])

            with pool.Fori(1, MID) as i:
                gather_four(i)

            pool.wait_ge(left_known, 1)
            with pool.If(pool.value_load(n_left_i[0:1, 0:1], min_val=0, max_val=E) > 0):
                with pool.Fori(0, NC) as c:
                    pool.wait_ge(g_ready, c + 1)
                    pool.nop(nofuse=True)
                    gather(scatter_idx, 0, g_gathered)
                pool.wait_ge(g_summed, NC * NB)
            with pool.Fori(MID, ITERS) as i:
                gather_four(i)

            pool.wait_ge(zeros_made, 2 * 16 * TABLES)

            def scatter(s, c, first):
                pool.wait_ge(scatter_idx_made, c + 1)
                pool.nop(nofuse=True)
                pool.wait_ge(merged_kept, c + 1)
                pool.nop(nofuse=True)
                for j in range(TPC):
                    k, turn = j % TABLES, j // TABLES
                    if not (first and turn == 0):
                        pool.wait_ge(table_free[k], c * (16 * TPC // TABLES) + 16 * turn)
                        pool.nop(nofuse=True)
                    pool.indirect_dma_start(tables[k], bass.IndirectOffsetOnAxis(ap=scatter_idx[:, s, j:j + 1], axis=0),
                                            att[:, s, j, :], None, compute_op=ALU.add).then_inc(table_free[k], 16)
                    if j == TABLES - 1:
                        pool.sem_inc(scattered, 1)

            for k in range(SLOTS):
                scatter((k + 2) % SLOTS, k, k == 0)
            with pool.Fori(1, ITERS) as i:
                for k in range(SLOTS):
                    scatter((k + 2) % SLOTS, SLOTS * i + k, False)

            for g in range(NG + 1):
                s, blocks = g % SLOTS, group_blocks(g)
                pool.wait_ge(tabs_loaded[s], 16 * TABLES * (g // SLOTS + 1))
                nc.gpsimd.tensor_tensor(tabs[g][:, 0:2, 0:blocks], tabs[g][:, 0:2, 0:blocks], tabs[g][:, 2:4, 0:blocks], ALU.add
                                        ).then_inc(tabs_halved, 1)
                if g % 2 == 0:
                    pool.wait_ge(tabs_halved, g + 1)
                    if g >= SLOTS:
                        pool.wait_ge(sums_turned, g + 1 - SLOTS)
                    nc.gpsimd.tensor_tensor(whole[s][:, 0:blocks], tabs[g][:, 0, 0:blocks], tabs[g][:, 1, 0:blocks], ALU.add
                                            ).then_inc(even_summed, 1)

        @block.scalar
        def _(act):
            for o, a in ((w_att_sb[:, 0:1], W_att[0:P]), (w_att_sb[:, 1:2], W_att[P:2 * P]),
                         (b_att_sb[:], b_att.rearrange("(o d) -> o d", o=1).to_broadcast([P, 1]))):
                act.dma_start(o, a).then_inc(att_loaded, 16)

            act.wait_ge(consts_made, 1)
            nc.scalar.activation(acc_w[:], ones[0:1, 0:1].to_broadcast([1, NPAD]), ACT.Copy, scale=0.0).then_inc(accs_zero, 1)

            act.wait_ge(att_loaded, 16 * 3)

            def keep_dst_term(q, t, width):
                act.wait_ge(dst_term_ps, t + 1)
                nc.scalar.activation(dst_term[:, bass.ds(t * AW, width)], ps[:, q, 0:width], ACT.Identity,
                                     bias=b_att_sb[:, 0:1]).then_inc(dst_term_sb, 1)

            with act.Fori(0, AS // 4) as i:
                for q in range(4):
                    keep_dst_term(q % 2, 4 * i + q, AW)
            keep_dst_term(0, AS, GW)

            def weights(q, src_terms, first_node, done):
                for j in range(TPC):
                    last = nc.scalar.activation(att[:, q, j, :], dst_term[:, bass.ds(first_node, P)], ACT.Sigmoid,
                                                bias=src_terms[:, j:j + 1])
                last.then_inc(done, 1)

            act.wait_ge(idx_made, 1)
            act.wait_ge(dst_term_sb, AS + 1)

            def weights_of_pairs(first, end):
                with act.Fori(first, end) as i:
                    for q in range(2):
                        c = 2 * i + q
                        node = act.value_load(base_i[0:1, bass.ds(c, 1)], min_val=0, max_val=N - 1)
                        act.wait_ge(src_term_made, c + 1)
                        weights(q, src_term[:, q], node, att_made)

            weights_of_pairs(0, 2)
            nc.scalar.activation(acc_in[:], ones[:, 0:1].to_broadcast([P, NPAD]), ACT.Copy, scale=0.0).then_inc(accs_zero, 1)
            weights_of_pairs(2, MID * SLOTS // 2)

            act.wait_ge(left_known, 1)
            with act.If(act.value_load(n_left_i[0:1, 0:1], min_val=0, max_val=E) > 0):
                with act.Fori(0, NC) as c:
                    with act.Fori(0, NB) as b:
                        act.wait_ge(g_hot, c * NB + b + 1)
                        weights(0, src_term[:, 0], b * P, g_att)

            def keep(s, c, first_quad):
                if not first_quad:
                    act.wait_ge(scattered, c - 2)
                act.wait_ge(merged, c + 1)
                for h in range(2):
                    last = nc.scalar.activation(att[:, s, 4 * h:4 * h + 4, :], merge_ps[:, 4 * h:4 * h + 4, :], ACT.Copy)
                last.then_inc(merged_kept, 1)

            for c in range(3):
                if c < 2:
                    keep(c + 2, c, True)
                weights_of_pairs(STOPS[c] * SLOTS // 2, STOPS[c + 1] * SLOTS // 2)
            act.wait_ge(hot_made, NC)
            keep(0, 2, True)
            keep(1, 3, True)
            act.wait_ge(by_dst_done, 1)

            def gru_head(t):
                act.wait_ge(agg_ps, t + 1)
                nc.scalar.activation(agg, agg_bank, ACT.Copy).then_inc(agg_sb, 1)

            def gru_gates(t, first):
                act.wait_ge(gates_ps, t + 1)
                if not first:
                    act.wait_ge(h_made, t)
                nc.scalar.activation(reset, reset_bank, ACT.Sigmoid, bias=b_gate[:, 0:1]).then_inc(reset_made, 1)
                nc.scalar.activation(update, update_bank, ACT.Sigmoid, bias=b_gate[:, 1:2]).then_inc(update_made, 1)

            def gru_new(t):
                act.wait_ge(pre_made, t + 1)
                nc.scalar.activation(new, pre, ACT.Tanh, bias=b_ih_sb[:, 2:3]).then_inc(new_made, 1)

            def pair_with_gru(p, h, first):
                gru_gates(p - 2, first)
                keep(2 * h, 2 * p, False)
                gru_new(p - 2)
                gru_head(p - 1)
                keep(2 * h + 1, 2 * p + 1, False)

            act.wait_ge(weights_made, 1)
            gru_head(0)
            pair_with_gru(2, 1, True)
            pair_with_gru(3, 0, False)
            with act.Fori(2, (GS + 1) // 2) as i:
                for h in range(2):
                    pair_with_gru(2 * i + h, 1 - h, False)
            gru_gates(GS - 1, False)
            gru_new(GS - 1)

            act.wait_ge(bn_made[0], 1)
            nc.scalar.activation(bn_std, bn_var, ACT.Sqrt, bias=eps[:, 0:1]).then_inc(bn_made[1], 1)
            act.wait_ge(bn_made[5], 1)

            u, std = agg, reset

            def keep_x1_part(t):
                act.wait_ge(x1_part_ps, t + 1)
                act.nop(nofuse=True)
                nc.scalar.activation(acc_x[:, bass.ds(t * GW, GW)], x1_part_bank, ACT.Identity, bias=bias_col[:, 0:1]
                                     ).then_inc(x1_part_kept, 1)

            def pair_with_ln(t, h, first):
                if not first:
                    act.wait_ge(y_made, t)
                nc.scalar.activation(u, acc_x[:, bass.ds(t * GW, GW)], ACT.Identity, scale=bn_scale, bias=bn_shift
                                     ).then_inc(u_made, 1)
                keep(2 * h, 2 * t + (2 * GS + 2), False)
                act.wait_ge(centered, t + 1)
                nc.scalar.activation(sq, center_bank, ACT.Square).then_inc(squared, 1)
                if not first:
                    keep_x1_part(t - 1)
                keep(2 * h + 1, 2 * t + (2 * GS + 3), False)
                act.wait_ge(var_ps, t + 1)
                if not first:
                    act.wait_ge(inv_made, t)
                nc.scalar.activation(std, var_bank, ACT.Sqrt, bias=eps[:, 0:1]).then_inc(std_made, 1)

            pair_with_ln(0, 1, True)
            with act.Fori(0, GS // 2) as i:
                for h in range(2):
                    pair_with_ln(2 * i + (h + 1), h, False)
            keep_x1_part(GS - 1)
            keep(0, NC - 2, False)
            keep(1, NC - 1, False)

            def keep_sums(g):
                h, blocks = g % 2, group_blocks(g)
                act.wait_ge(sums_turned, g + 1)
                if g >= 2:
                    act.wait_ge(out_ps, g - 1)
                nc.scalar.activation(sums_T[:, h, 0:blocks], summed_T[h][:, 0:blocks], ACT.Copy).then_inc(sums_kept, 1)

            def out_std(g):
                s, blocks = g % SLOTS, group_blocks(g)
                act.wait_ge(o_mv_made, g + 1)
                nc.scalar.activation(o_std[:, s, 0:blocks], o_mv[:, s, 0:blocks, 1], ACT.Sqrt, bias=eps[:, 0:1]
                                     ).then_inc(o_std_made, 1)

            def norm(g):
                s, r, blocks = g % SLOTS, g % len(out_rows), group_blocks(g)
                act.wait_ge(o_shift_made, g + 1)
                for b in range(blocks):
                    last = nc.scalar.activation(out_rows[r][:, b], out_rows[r][:, b], ACT.Identity,
                                                scale=o_inv[:, s, b:b + 1], bias=o_shift[:, s, b:b + 1])
                last.then_inc(o_made, 1)

            keep_sums(0)
            keep_sums(1)
            for g in range(NG + 1):
                if g + 2 <= NG:
                    keep_sums(g + 2)
                out_std(g)
                if g >= 1:
                    norm(g - 1)
            norm(NG)

        @block.vector
        def _(dve):
            v = nc.vector
            v.memset(ones[:], 1.0)
            v.memset(mean_w[:], 1.0 / P)
            v.memset(eps[:], EPS)
            dve.wait_ge(iotas_made, 1)
            v.tensor_copy(col[:], iota_i[:])
            v.tensor_copy(part[:], part_i[:]).then_inc(consts_made, 1)
            dve.wait_ge(consts_made, 1)
            v.tensor_scalar(ident[:], col[:], part[:, 0:1], None, ALU.is_equal)
            v.tensor_scalar(earlier[:], col[:], part[:, 0:1], None, ALU.is_lt)
            v.tensor_scalar(trash_row[:], part[:], float(TRASH), None, ALU.add).then_inc(consts_made, 1)
            dve.wait_ge(consts_made, 2)
            v.tensor_tensor(center[:], ident[:], mean_w[:], ALU.subtract).then_inc(consts_made, 1)

            dve.wait_ge(att_loaded, 16 * 3)
            v.tensor_scalar(diag[:], ident[:], w_att_sb[:, 0:1], None, ALU.mult).then_inc(att_diag_made, 1)
            dve.wait_ge(att_spread, 1)
            v.tensor_copy(w_att_a[:], spread_ps).then_inc(att_kept, 1)

            dve.wait_ge(idx_loaded, 64)
            v.tensor_copy(src_rows, src_rows_i)
            v.tensor_copy(base_col, dst_rows_i[:, 0:1]).then_inc(rows_made, 1)
            v.tensor_scalar(mask_rows, mask_i, 0.0, None, ALU.is_lt).then_inc(rows_made, 1)
            dve.wait_ge(rows_made, 2)
            v.tensor_scalar(rel_rows, dst_rows_i, base_col, None, ALU.subtract)
            v.tensor_tensor(key_rows, number_i, src_rows, ALU.subtract).then_inc(rows_made, 1)
            dve.wait_ge(rows_turned, 1)
            for h in range(2):
                v.tensor_copy(gather_all[:, 0:NC, 4 * h:4 * h + 4].rearrange("p c j -> p j c"), turned[:, h]).then_inc(idx_kept, 1)
            dve.wait_ge(rows_made, 3)
            v.scalar_tensor_tensor(rel_rows, mask_rows, FAR, rel_rows, ALU.mult, ALU.add)
            v.tensor_tensor(key_rows, key_rows, mask_rows, ALU.mult).then_inc(rows_made, 1)
            dve.wait_ge(rows_made, 4)
            v.tensor_tensor(key_rows, key_rows, src_rows, ALU.add).then_inc(rows_made, 1)
            v.memset(dst_term[:, N:NPAD], 0.0)
            v.memset(key[:, NC:NC + 2], 0.0)
            v.memset(gather_all[:, NC:NC + SLOTS], 0)
            dve.wait_ge(rows_turned, 2)
            v.tensor_copy(base_i[:], base_ps)
            for a, kept in ((1, rel), (2, key)):
                for h in range(2):
                    last = v.tensor_copy(kept[:, 0:NC, 4 * h:4 * h + 4].rearrange("p c j -> p j c"), turned[:, 2 * a + h])
            last.then_inc(idx_made, 1)

            dve.wait_ge(idx_made, 1)
            def src_products(s, product, o, done):
                for j in range(TPC):
                    last = v.tensor_tensor_reduce(product[:, j], rows[:, s, j, :], w_att_a[:], 1.0, 0.0, ALU.mult, ALU.add,
                                                  o[:, j:j + 1])
                last.then_inc(done, 1)

            def src_terms(s, i, c):
                dve.wait_ge(gathered[s], i * (16 * TPC) + 16 * TPC)
                v.tensor_copy(gather_idx[:, s], chunk_of(gather_all, c + SLOTS)).then_inc(gather_idx_made, 1)
                src_products(s, (dups, same)[s % 2], src_term[:, s % 2], src_term_made)

            def weigh(q, c):
                dve.wait_ge(att_made, c + 1)
                for j in range(TPC):
                    last = v.scalar_tensor_tensor(hot[:, q, j, :], col[:], rel[:, bass.ds(c, 1), j:j + 1].rearrange("p c j -> p (c j)"),
                                                  att[:, q, j, :], ALU.is_equal, ALU.mult)
                last.then_inc(hot_made, 1)

            def add_sums(q, c, first):
                node = dve.value_load(base_i[0:1, bass.ds(c, 1)], min_val=0, max_val=N - 1)
                dve.wait_ge(summed, c + 1)
                if first:
                    dve.wait_ge(acc_x_zero, 1)
                    dve.wait_ge(accs_zero, 1)
                else:
                    dve.wait_ge(added, c)
                v.tensor_tensor(acc_x[:, bass.ds(node, P)], acc_x[:, bass.ds(node, P)], sum_ps[q], ALU.add)
                v.tensor_tensor(acc_w[:, bass.ds(node, P)], acc_w[:, bass.ds(node, P)], weight_ps[q], ALU.add).then_inc(added, 1)

            def first_loop(i, first, n_merged):
                for s in range(SLOTS):
                    src_terms(s, i, SLOTS * i + s)
                    if s == 0 and n_merged:
                        dve.wait_ge(merged, n_merged)
                    if first and s == 0:
                        v.memset(acc_x[:], 0.0).then_inc(acc_x_zero, 1)
                    if s >= 1:
                        weigh((s - 1) % 2, SLOTS * i + s - 1)
                    if s >= 2:
                        add_sums(s % 2, SLOTS * i + s - 2, first and s == 2)
                weigh(1, SLOTS * i + 3)
                add_sums(0, SLOTS * i + 2, False)
                add_sums(1, SLOTS * i + 3, False)

            dve.wait_ge(att_kept, 1)
            dve.wait_ge(idx_kept, 2)
            first_loop(0, True, 0)
            dve.wait_ge(w_loaded, 16 * len(small_loads))
            v.tensor_tensor(b_gate[:], b_ih_sb[:, 0:2], b_hh_sb[:, 0:2], ALU.add)
            v.tensor_tensor(w_node_sb[:], w_node_sb[:], ident[:], ALU.add)
            v.tensor_scalar(left, rel[:], float(P), None, ALU.is_ge).then_inc(left_step, 1)
            dve.wait_ge(left_step, 1)
            v.scalar_tensor_tensor(left, rel[:], FAR / 2, left, ALU.is_lt, ALU.mult).then_inc(left_step, 1)
            dve.wait_ge(left_step, 2)
            v.scalar_tensor_tensor(left, rel[:], 0.0, left, ALU.is_lt, ALU.add).then_inc(left_step, 1)
            dve.wait_ge(left_step, 3)
            v.tensor_reduce(n_left[:], left, AX.XY, ALU.add).then_inc(left_step, 1)
            dve.wait_ge(left_counted, 1)
            v.tensor_tensor(bias_col[:], bias_ps, vecs[:, 3:4], ALU.add).then_inc(weights_made, 1)
            v.tensor_copy(n_left_i[:], left_ps).then_inc(left_known, 1)
            with dve.Fori(1, MID) as i:
                first_loop(i, False, 0)

            def tiles(ap):
                return ap.unsqueeze(2).to_broadcast([P, TPC, P])

            def every(ap):
                return ap.unsqueeze(1).to_broadcast([P, TPC, P])

            dve.wait_ge(zeros_made, 2 * 16 * TABLES)

            dve.wait_ge(left_known, 1)
            with dve.If(dve.value_load(n_left_i[0:1, 0:1], min_val=0, max_val=E) > 0):
                dve.wait_ge(added, SLOTS * MID)
                v.tensor_copy(base_f, base_i[:]).then_inc(g_base, 1)
                dve.wait_ge(g_base_ps, 1)
                v.tensor_copy(base_bc, base_bc_ps).then_inc(g_base, 1)
                dve.wait_ge(g_base, 2)
                with dve.Fori(0, NC) as c:
                    v.tensor_copy(scatter_idx[:, 0], chunk_of(gather_all, c))
                    v.tensor_scalar(left_now, chunk_of(rel, c), base_bc[:, bass.ds(c, 1)], 1.0, ALU.add, ALU.add).then_inc(g_left, 1)
                    dve.wait_ge(g_left, 3 * c + 1)
                    v.tensor_tensor(left_now, left_now, chunk_of(left, c), ALU.mult).then_inc(g_left, 1)
                    dve.wait_ge(g_left, 3 * c + 2)
                    v.tensor_scalar(left_now, left_now, -1.0, None, ALU.add).then_inc(g_left, 1)
                    dve.wait_ge(g_left, 3 * c + 3)
                    v.tensor_copy(n_dups[:], left_now).then_inc(g_ready, 1)
                    dve.wait_ge(g_gathered, c * (16 * TPC) + 16 * TPC)
                    src_products(0, same, src_term[:, 0], g_src_term)
                    dve.wait_ge(g_src_term, c + 1)
                    dve.nop(nofuse=True)
                    with dve.Fori(0, NB) as b:
                        n = c * NB + b
                        v.tensor_tensor(hot[:, 0], every(col[:]), tiles(left_now), ALU.is_equal).then_inc(g_hot, 1)
                        dve.wait_ge(g_att, n + 1)
                        dve.wait_ge(g_hot, n + 1)
                        v.tensor_tensor(hot[:, 1], hot[:, 0], att[:, 0], ALU.mult)
                        v.tensor_scalar(left_now, left_now, -float(P), None, ALU.add).then_inc(g_weighted, 1)
                        dve.wait_ge(g_summed, n + 1)
                        for acc, bank in ((acc_x, sum_ps[0]), (acc_w, weight_ps[0]), (acc_in, sum_ps[1])):
                            last = v.tensor_tensor(acc[:, bass.ds(b * P, P)], acc[:, bass.ds(b * P, P)], bank, ALU.add)
                        last.then_inc(g_added, 1)
                        dve.wait_ge(g_added, n + 1)
            v.memset(n_dups[:], 0.0).then_inc(general_done, 1)
            dve.wait_ge(general_done, 1)

            def copy_keys(q, c):
                v.tensor_copy(key_now[:, q], chunk_of(key, c)).then_inc(keys_copied, 1)

            def find(q, s, c, first, second, first_quad):
                v.tensor_tensor(hot[:, q], every(col[:]), tiles(chunk_of(rel, c)), ALU.is_equal).then_inc(onehot_made, 1)
                if not first:
                    add_in(c - 1, second)
                dve.wait_ge(keys_spread, c + 1)
                if not first:
                    dve.wait_ge(merged, c)
                v.tensor_tensor(same[:], key_ps, tiles(chunk_of(key, c)), ALU.is_equal).then_inc(same_made, 1)
                dve.wait_ge(same_made, c + 1)
                v.tensor_tensor(dups[:], same[:], every(earlier[:]), ALU.mult).then_inc(dups_made, 1)
                copy_keys(q, c + 2)
                v.tensor_scalar(to_trash[:], chunk_of(key, c), -1.0, trash_row[:, 0:1], ALU.mult, ALU.add)
                dve.wait_ge(dups_made, c + 1)
                v.tensor_reduce(n_dups[:], dups[:], AX.X, ALU.add).then_inc(counted, 1)
                dve.wait_ge(counted, c + 1)
                v.scalar_tensor_tensor(moved[:], n_dups[:], 1.0, to_trash[:], ALU.min, ALU.mult).then_inc(moved_made, 1)
                dve.wait_ge(moved_made, c + 1)
                if not first_quad:
                    dve.wait_ge(scattered, c - 2)
                v.tensor_tensor(scatter_idx[:, s], moved[:], chunk_of(key, c), ALU.add).then_inc(scatter_idx_made, 1)

            def add_in(c, first):
                node = dve.value_load(base_i[0:1, bass.ds(c, 1)], min_val=0, max_val=N - 1)
                dve.wait_ge(in_summed, c + 1)
                if not first:
                    dve.wait_ge(in_added, c)
                v.tensor_tensor(acc_in[:, bass.ds(node, P)], acc_in[:, bass.ds(node, P)], in_ps, ALU.add
                                ).then_inc(in_added, 1)

            def pair(p, h, first, first_quad):
                find(0, 2 * h, 2 * p, first, False, first_quad)
                find(1, 2 * h + 1, 2 * p + 1, False, first, first_quad)

            copy_keys(0, 0)
            copy_keys(1, 1)
            for c in range(3):
                find(c % 2, (c + 2) % SLOTS, c, c == 0, c == 1, True)
                with dve.Fori(STOPS[c], STOPS[c + 1]) as i:
                    first_loop(i, False, c + 1)
            dve.wait_ge(added, NC)
            v.memset(n_dups[:], 0.0).then_inc(by_dst_done, 1)
            dve.wait_ge(by_dst_done, 1)

            def gru_pre(t):
                dve.wait_ge(reset_made, t + 1)
                v.scalar_tensor_tensor(tmp, new_h_bank, b_hh_sb[:, 2:3], reset, ALU.add, ALU.mult).then_inc(scaled, 1)
                dve.wait_ge(scaled, t + 1)
                v.tensor_tensor(pre, tmp, new_in_bank, ALU.add).then_inc(pre_made, 1)

            def gru_mix(t):
                nodes = bass.ds(t * GW, GW)
                dve.wait_ge(new_made, t + 1)
                v.tensor_tensor(tmp, xT_sb[:, nodes], new, ALU.subtract).then_inc(diff_made, 1)
                dve.wait_ge(diff_made, t + 1)
                dve.wait_ge(update_made, t + 1)
                v.tensor_tensor(tmp, tmp, update, ALU.mult).then_inc(mixed, 1)
                dve.wait_ge(mixed, t + 1)
                v.tensor_tensor(acc_x[:, nodes], tmp, new, ALU.add).then_inc(h_made, 1)
                dve.wait_ge(h_made, t + 1)
                v.bn_stats(stats[:, bass.ds(t * 6, 6)], acc_x[:, nodes]).then_inc(bn_stats_made, 1)

            def pair_with_gru(p, h):
                find(0, 2 * h, 2 * p, False, False, False)
                gru_pre(p - 2)
                find(1, 2 * h + 1, 2 * p + 1, False, False, False)
                gru_mix(p - 2)

            find(1, 1, 3, False, False, True)
            with dve.Fori(1, (GS + 1) // 2) as i:
                for h in range(2):
                    pair_with_gru(2 * i + h, 1 - h)
            gru_pre(GS - 1)
            gru_mix(GS - 1)

            dve.wait_ge(bn_stats_made, GS)
            v.bn_aggr(bn[:, 0:2], stats[:]).then_inc(bn_made[0], 1)
            dve.wait_ge(bn_made[1], 1)
            v.reciprocal(bn_inv, bn_std).then_inc(bn_made[2], 1)
            dve.wait_ge(bn_made[2], 1)
            v.tensor_tensor(bn_scale, bn_inv, vecs[:, 0:1], ALU.mult).then_inc(bn_made[3], 1)
            dve.wait_ge(bn_made[3], 1)
            v.tensor_tensor(bn_off, bn_mean, bn_scale, ALU.mult).then_inc(bn_made[4], 1)
            dve.wait_ge(bn_made[4], 1)
            v.tensor_tensor(bn_shift, vecs[:, 1:2], bn_off, ALU.subtract).then_inc(bn_made[5], 1)

            u, std, inv = agg, reset, tmp

            def ln_finish(t):
                dve.wait_ge(std_made, t + 1)
                v.reciprocal(inv, std).then_inc(inv_made, 1)
                dve.wait_ge(inv_made, t + 1)
                v.tensor_tensor(acc_x[:, bass.ds(t * GW, GW)], center_bank, inv, ALU.mult).then_inc(x1_made, 1)

            def pair_with_ln(t, h, first):
                p = t + (GS + 1)
                dve.wait_ge(u_made, t + 1)
                if not first:
                    dve.wait_ge(centered, t)
                v.tensor_tensor(y, u, xT_sb[:, bass.ds(t * GW, GW)], ALU.add).then_inc(y_made, 1)
                find(0, 2 * h, 2 * p, False, False, False)
                if not first:
                    ln_finish(t - 1)
                find(1, 2 * h + 1, 2 * p + 1, False, False, False)

            pair_with_ln(0, 1, True)
            with dve.Fori(0, GS // 2) as i:
                for h in range(2):
                    pair_with_ln(2 * i + (h + 1), h, False)
            ln_finish(GS - 1)
            pair(PAIRS - 1, 0, False, False)
            add_in(NC - 1, False)

            def add_in_part(h, g, blocks):
                dve.wait_ge(in_part_ps, g + 1)
                v.tensor_tensor(z_sb[:, h, 0:blocks], ps[:, h, 0:blocks * P].rearrange("p (b f) -> p b f", f=P),
                                acc_x[:, bass.ds(g * (GROUP * P), blocks * P)].rearrange("p (b f) -> p b f", f=P), ALU.add
                                ).then_inc(z_made, 1)

            def keep_z(h, g, blocks):
                dve.wait_ge(z_turned, g + 1)
                v.tensor_copy(by_node[:, bass.ds(g * GROUP, blocks)], turned_z[h][:, 0:blocks]).then_inc(z_kept, 1)

            dve.wait_ge(x1_part_kept, GS)
            with dve.Fori(0, NG // 2) as i:
                for step in (add_in_part, keep_z):
                    for h in range(2):
                        step(h, 2 * i + h, GROUP)
            add_in_part(0, NG, 1)
            keep_z(0, NG, 1)

            def sum_halves(g):
                s = g % SLOTS
                dve.wait_ge(tabs_halved, g + 1)
                if g >= SLOTS:
                    dve.wait_ge(sums_turned, g + 1 - SLOTS)
                v.tensor_tensor(whole[s], tabs[g][:, 0], tabs[g][:, 1], ALU.add).then_inc(odd_summed, 1)

            def scale(g):
                s, blocks = g % SLOTS, group_blocks(g)
                dve.wait_ge(o_std_made, g + 1)
                v.reciprocal(o_inv[:, s, 0:blocks], o_std[:, s, 0:blocks]).then_inc(o_inv_made, 1)

            def shift(g):
                s, blocks = g % SLOTS, group_blocks(g)
                dve.wait_ge(o_inv_made, g + 1)
                v.scalar_tensor_tensor(o_shift[:, s, 0:blocks], o_mv[:, s, 0:blocks, 0], -1.0, o_inv[:, s, 0:blocks],
                                       ALU.mult, ALU.mult).then_inc(o_shift_made, 1)

            sum_halves(1)
            dve.wait_ge(z_kept, NG + 1)
            for g in range(NG + 1):
                s, h, r, blocks = g % SLOTS, g % 2, g % len(out_rows), group_blocks(g)
                dve.wait_ge(out_ps, g + 1)
                if g >= SLOTS:
                    dve.wait_ge(o_made, g + 1 - SLOTS)
                if g >= len(out_rows):
                    dve.wait_ge(stored[r], 16 * (g // len(out_rows)))
                v.tensor_tensor(out_rows[r][:, 0:blocks], out_bank[h][:, 0:blocks], by_node[:, g * GROUP:g * GROUP + blocks], ALU.add
                                ).then_inc(o_added, 1)
                if g >= 1:
                    scale(g - 1)
                dve.wait_ge(o_added, g + 1)
                for b in range(blocks):
                    last = v.bn_stats(o_stat[:, s, b], out_rows[r][:, b])
                last.then_inc(o_stats_made, 1)
                if g >= 1:
                    shift(g - 1)
                dve.wait_ge(o_stats_made, g + 1)
                dve.nop(nofuse=True)
                for b in range(blocks):
                    last = v.bn_aggr(o_mv[:, s, b], o_stat[:, s, b])
                last.then_inc(o_mv_made, 1)
                if g % 2 == 0 and g + 3 < NG:
                    sum_halves(g + 3)
            scale(NG)
            shift(NG)

        @block.tensor
        def _(pe):
            mm = nc.tensor.matmul

            def turn(a, by_chunk):
                tile = by_chunk.rearrange("c (p j) -> c j p", j=TPC)
                for j in range(TPC):
                    last = nc.tensor.transpose(turned[:, 2 * a + j // 4, j % 4], tile[:, j], ident[0:NC, 0:NC])
                return last

            pe.wait_ge(consts_made, 3)
            pe.wait_ge(att_diag_made, 1)
            mm(spread_ps, ones[:], diag[:], start=True, stop=True).then_inc(att_spread, 1)

            pe.wait_ge(rows_made, 1)
            turn(0, src_rows).then_inc(rows_turned, 1)
            pe.wait_ge(x_loaded[0], 16)
            pe.wait_ge(idx_kept, 2)

            def dst_terms(q, t, width):
                mm(ps[:, q, 0:width], w_att_sb[:, 1:2].to_broadcast([P, P]), xT_sb[:, bass.ds(t * AW, width)],
                   start=True, stop=True).then_inc(dst_term_ps, 1)

            def dst_terms_of_pairs(first, end):
                with pe.Fori(first, end) as i:
                    for q in range(2):
                        pe.wait_ge(dst_term_sb, 2 * i + (q - 1))
                        dst_terms(q, 2 * i + q, AW)

            dst_terms(0, 0, AW)
            dst_terms(1, 1, AW)
            dst_terms_of_pairs(1, X_SPLIT // 2)

            pe.wait_ge(rows_made, 5)
            nc.tensor.transpose(base_ps, base_col, ident[0:NC, 0:NC])
            turn(1, rel_rows)
            turn(2, key_rows).then_inc(rows_turned, 1)

            pe.wait_ge(x_loaded[1], 16)
            dst_terms_of_pairs(X_SPLIT // 2, AS // 2)
            pe.wait_ge(dst_term_sb, AS - 1)
            dst_terms(0, AS, GW)
            pe.wait_ge(dst_term_sb, AS + 1)

            def window_sum(bank, values, weights):
                for j in range(TPC):
                    last = mm(bank, values(j), weights[:, j, :], start=(j == 0), stop=(j == TPC - 1))
                return last

            pe.wait_ge(idx_made, 1)
            def sums(i):
                for s in range(SLOTS):
                    q = s % 2
                    pe.wait_ge(hot_made, SLOTS * i + s + 1)
                    window_sum(sum_ps[q], lambda j: rows[:, s, j, :], hot[:, q]).then_inc(rows_used, 1)
                    window_sum(weight_ps[q], lambda j: ones[:, 0:1], hot[:, q]).then_inc(summed, 1)

            sums(0)
            pe.wait_ge(w_loaded, 16 * len(small_loads))
            mm(bias_ps, w_glob_sb[:], vecs[:, 2:3], start=True, stop=True)
            pe.wait_ge(left_step, 4)
            mm(left_ps, n_left[:], ones[:, 0:1], start=True, stop=True).then_inc(left_counted, 1)
            with pe.Fori(1, MID) as i:
                sums(i)

            pe.wait_ge(left_known, 1)
            with pe.If(pe.value_load(n_left_i[0:1, 0:1], min_val=0, max_val=E) > 0):
                pe.wait_ge(g_base, 1)
                mm(base_bc_ps, ones[0:1, :], base_f, start=True, stop=True).then_inc(g_base_ps, 1)
                with pe.Fori(0, NC) as c:
                    pe.wait_ge(g_loaded, 16 * c + 16)
                    pe.nop(nofuse=True)
                    with pe.Fori(0, NB) as b:
                        pe.wait_ge(g_weighted, c * NB + b + 1)
                        window_sum(sum_ps[0], lambda j: rows[:, 0, j, :], hot[:, 1])
                        window_sum(weight_ps[0], lambda j: ones[:, 0:1], hot[:, 1])
                        window_sum(sum_ps[1], lambda j: ea[:, 0, j, :], hot[:, 0]).then_inc(g_summed, 1)

            def spread_keys(q, c):
                pe.wait_ge(keys_copied, c + 1)
                for j in range(TPC):
                    last = nc.tensor.transpose(key_ps[:, j], key_now[:, q, j:j + 1].to_broadcast([P, P]), ident[:])
                last.then_inc(keys_spread, 1)

            def chunk(q, i, first):
                c = 2 * i + q
                pe.wait_ge(ea_loaded[q], 16 * i + 16)
                pe.wait_ge(onehot_made, c + 1)
                if not first:
                    pe.wait_ge(in_added, c)
                window_sum(in_ps, lambda j: ea[:, q, j, :], hot[:, q]).then_inc(in_summed, 1)
                pe.wait_ge(same_made, c + 1)
                spread_keys(1 - q, c + 1)
                if not first:
                    pe.wait_ge(merged_kept, c)
                for j in range(TPC):
                    last = mm(merge_ps[:, j], same[:, j, :], ea[:, q, j, :], start=True, stop=True)
                last.then_inc(merged, 1)

            spread_keys(0, 0)
            for c in range(3):
                chunk(c % 2, c // 2, c == 0)
                with pe.Fori(STOPS[c], STOPS[c + 1]) as i:
                    sums(i)

            def gru_agg(t, first):
                nodes = bass.ds(t * GW, GW)
                if not first:
                    pe.wait_ge(reset_made, t)
                mm(agg_bank, w_msg_sb[:], acc_x[:, nodes], start=True, stop=False)
                mm(agg_bank, b_msg_row[:], acc_w[:, nodes], start=False, stop=True).then_inc(agg_ps, 1)

            def gru_gates(t, first):
                nodes = bass.ds(t * GW, GW)
                pe.wait_ge(agg_sb, t + 1)
                if not first:
                    pe.wait_ge(pre_made, t)
                    pe.wait_ge(update_made, t)
                for g, bank in enumerate((reset_bank, update_bank)):
                    mm(bank, w_ih_sb[:, g * P:(g + 1) * P], agg, start=True, stop=False)
                    mm(bank, w_hh_sb[:, g * P:(g + 1) * P], xT_sb[:, nodes], start=False, stop=True)
                mm(new_in_bank, w_ih_sb[:, 2 * P:], agg, start=True, stop=True)
                mm(new_h_bank, w_hh_sb[:, 2 * P:], xT_sb[:, nodes], start=True, stop=True).then_inc(gates_ps, 1)

            def pair_with_gru(i):
                chunk(0, i, False)
                gru_agg(i - 1, False)
                chunk(1, i, False)
                gru_gates(i - 1, False)

            pe.wait_ge(weights_made, 1)
            chunk(1, 1, False)
            pe.wait_ge(by_dst_done, 1)
            gru_agg(0, True)
            gru_gates(0, True)
            with pe.Fori(2, GS + 1) as i:
                pair_with_gru(i)

            def project_x1(t, first):
                pe.wait_ge(x1_made, t + 1)
                if not first:
                    pe.wait_ge(x1_part_kept, t)
                mm(x1_part_bank, w_node_sb[:], acc_x[:, bass.ds(t * GW, GW)], start=True, stop=True).then_inc(x1_part_ps, 1)

            def pair_with_ln(t, first, second):
                chunk(0, t + (GS + 1), False)
                pe.wait_ge(y_made, t + 1)
                if not first:
                    pe.wait_ge(x1_made, t)
                mm(center_bank, center[:], y, start=True, stop=True).then_inc(centered, 1)
                if not first:
                    project_x1(t - 1, second)
                chunk(1, t + (GS + 1), False)
                pe.wait_ge(squared, t + 1)
                mm(var_bank, mean_w[:], sq, start=True, stop=True).then_inc(var_ps, 1)

            pe.wait_ge(pre_made, GS)
            pe.wait_ge(update_made, GS)
            pair_with_ln(0, True, False)
            pair_with_ln(1, False, True)
            with pe.Fori(2, GS) as t:
                pair_with_ln(t, False, False)
            project_x1(GS - 1, False)
            chunk(0, PAIRS - 1, False)
            chunk(1, PAIRS - 1, False)

            def project_in(h, g, blocks, first):
                if not first:
                    pe.wait_ge(z_made, g - 1)
                mm(ps[:, h, 0:blocks * P], w_in_sb[:], acc_in[:, bass.ds(g * (GROUP * P), blocks * P)],
                   start=True, stop=True).then_inc(in_part_ps, 1)

            def turn_z(h, g, blocks, first):
                pe.wait_ge(z_made, g + 1)
                if not first:
                    pe.wait_ge(z_kept, g - 1)
                for b in range(blocks):
                    last = nc.tensor.transpose(turned_z[h][:, b], z_sb[:, h, b], ident[:])
                last.then_inc(z_turned, 1)

            def two_groups(i, first):
                for step in (project_in, turn_z):
                    for h in range(2):
                        step(h, 2 * i + h, GROUP, first)

            pe.wait_ge(in_added, NC)
            pe.wait_ge(same_made, NC)
            pe.wait_ge(x1_part_kept, GS)
            two_groups(0, True)
            with pe.Fori(1, NG // 2) as i:
                two_groups(i, False)
            project_in(0, NG, 1, False)
            turn_z(0, NG, 1, False)

            def turn_sums(g):
                s, h, blocks = g % SLOTS, g % 2, group_blocks(g)
                pe.wait_ge((even_summed, odd_summed)[h], g // 2 + 1)
                if g >= 2:
                    pe.wait_ge(sums_kept, g - 1)
                for b in range(blocks):
                    last = nc.tensor.transpose(summed_T[h][:, b], whole[s][:, b], ident[:])
                last.then_inc(sums_turned, 1)

            pe.wait_ge(merged_kept, NC)
            turn_sums(0)
            for g in range(NG + 1):
                h, blocks = g % 2, group_blocks(g)
                if 1 <= g < NG:
                    turn_sums(g + 1)
                pe.wait_ge(sums_kept, g + 1)
                if g >= 2:
                    pe.wait_ge(o_added, g - 1)
                for b in range(blocks):
                    last = mm(out_bank[h][:, b], sums_T[:, h, b], w_out_sb[:], start=True, stop=True)
                last.then_inc(out_ps, 1)
                if g == 0:
                    turn_sums(1)


def kernel(**inputs):
    import numpy as np
    import concourse.bacc as bacc
    from concourse.bass_utils import run_bass_kernel_spmd

    a = {k: np.asarray(v) for k, v in inputs.items()}
    order = {
        "x": a["x"], "xT": a["x"].T, "src": a["src"], "dst": a["dst"], "edge_attr": a["edge_attr_128"],
        "W_msg": a["L0_gnn_W_msg"], "b_msg": a["L0_gnn_b_msg"], "W_att": a["L0_gnn_W_att"], "b_att": a["L0_gnn_b_att"],
        "W_ihT": a["L0_gnn_W_ih"].T, "b_ih": a["L0_gnn_b_ih"], "W_hhT": a["L0_gnn_W_hh"].T, "b_hh": a["L0_gnn_b_hh"],
        "gamma": a["L0_gnn_gamma"], "beta": a["L0_gnn_beta"], "glob": a["L1_gnn_global_features"],
        "W_nodeT": a["L1_gnn_W_node"].T, "W_inT": a["L1_gnn_W_incoming"].T, "W_outT": a["L1_gnn_W_outgoing"].T,
        "W_globT": a["L1_gnn_W_global"].T, "bias": a["L1_gnn_bias"],
    }
    nc = bacc.Bacc("TRN2", target_bir_lowering=False, num_devices=1)
    arrays, args = {}, []
    for name, v in order.items():
        v = np.ascontiguousarray(v)
        arrays[f"in_{name}"] = v
        args.append(nc.dram_tensor(f"in_{name}", v.shape, mybir.dt.from_np(v.dtype), kind="ExternalInput").ap())
    args.append(nc.dram_tensor("out_x", a["x"].shape, F32, kind="ExternalOutput").ap())
    gnn_two_layers(nc, *args)
    r = run_bass_kernel_spmd(nc, [arrays], core_ids=[0])
    return r.results[0]["out_x"]
```
